# Optimizing a Trainium2 kernel written in Bass

```python
import numpy as np
import jax
import jax.numpy as jnp

def _softmax(x, axis=-1):
    return jax.nn.softmax(x, axis=axis)

def _gelu(x):
    return jax.nn.gelu(x, approximate=True)

def _silu(x):
    return jax.nn.silu(x)

def _sigmoid(x):
    return jax.nn.sigmoid(x)

def _layernorm(x, axis=-1, eps=1e-05):
    m = jnp.mean(x, axis=axis, keepdims=True)
    v = jnp.var(x, axis=axis, keepdims=True)
    return (x - m) / jnp.sqrt(v + eps)

def _scatter_add(tgt, idx, src, axis=0):
    return tgt.at[idx].add(src)

def _segment_sum(src, seg, n):
    return jax.ops.segment_sum(src, seg, n)
kernel_name = 'mk_conv_seq_d1_conv_nhwc192_r2_188ace'

def setup_inputs(seed: int=0):
    np.random.seed(seed)
    _w = jnp.asarray

    def _rec_inputs():
        import jax
        import jax.numpy as jnp
        _gk = jax.random.key(seed)
        x = -0.0002221 + 1 * jax.random.normal(jax.random.fold_in(_gk, 1), (8, 64, 64, 96), jnp.float32)
        return x
    x = _rec_inputs()

    def _L0_conv_setup():
        import jax, jax.numpy as jnp
        import numpy as np
        B, HH, WW, E = (8, 64, 64, 96)
        NH = 8
        D1 = 3 * E // NH * NH
        HD = D1 // NH
        RPE = 256
        LAYERS = 3
        EPS = 1e-08

        def srms(x):
            d = x.shape[-1]
            norm = jnp.linalg.norm(x, axis=-1, keepdims=True)
            return x / (norm * d ** (-0.5) + EPS)

        def rpe_net(idx, pos_w, pos_b, lw, lb, out_w, out_b):
            h = idx @ pos_w.T + pos_b
            for i in range(LAYERS):
                h = jax.nn.relu(srms(h)) @ lw[i].T + lb[i]
            h = jax.nn.relu(srms(h)) @ out_w.T + out_b
            return h.reshape(idx.shape[0], NH, HD).transpose(1, 0, 2)

        def tno(v, axis, pos_w, pos_b, lw, lb, out_w, out_b):
            n = v.shape[axis]
            z = jnp.zeros((1,), jnp.float32)
            p = jnp.arange(1, n, dtype=jnp.float32)
            idx = jnp.concatenate([z, p, z, -p[::-1]]).reshape(-1, 1)
            a = rpe_net(idx, pos_w, pos_b, lw, lb, out_w, out_b)
            ak = a[:, None, :, :] if axis == -2 else a[:, :, None, :]
            y = jnp.fft.rfft(v, 2 * n, axis=axis)
            af = jnp.fft.rfft(ak, 2 * n, axis=axis)
            out = jnp.fft.irfft(af * y, 2 * n, axis=axis)
            return out[..., :n, :] if axis == -2 else out[..., :n, :, :]
        key = jax.random.key(seed)
        ks = jax.random.split(key, 19)
        s = 0.02
        rn = lambda k, shape, sc=s: jax.random.normal(k, shape, dtype=jnp.float32) * sc
        inp = {'x': jax.random.normal(ks[0], (B, HH, WW, E), dtype=jnp.float32), 'u_w': rn(ks[1], (D1, E)), 'u_b': rn(ks[2], (D1,)), 'v_w': rn(ks[3], (D1, E)), 'v_b': rn(ks[4], (D1,)), 'o_w': rn(ks[5], (E, D1)), 'o_b': rn(ks[6], (E,))}
        for i, name in enumerate(['rpe1', 'rpe2']):
            off = 7 + i * 6
            inp[name + '_pos_w'] = rn(ks[off], (RPE, 1), 0.5)
            inp[name + '_pos_b'] = rn(ks[off + 1], (RPE,), 0.5)
            inp[name + '_lw'] = rn(ks[off + 2], (LAYERS, RPE, RPE))
            inp[name + '_lb'] = rn(ks[off + 3], (LAYERS, RPE))
            inp[name + '_out_w'] = rn(ks[off + 4], (NH * HD, RPE))
            inp[name + '_out_b'] = rn(ks[off + 5], (NH * HD,))
        inp['H'] = HH
        inp['W'] = WW
        return inp
    _L0_conv_all = _L0_conv_setup()
    _L0_conv_in = {k: v for k, v in _L0_conv_all.items() if k in ('u_w', 'u_b', 'v_w', 'v_b', 'o_w', 'o_b', 'rpe1_pos_w', 'rpe1_pos_b', 'rpe1_lw', 'rpe1_lb', 'rpe1_out_w', 'rpe1_out_b', 'rpe2_pos_w', 'rpe2_pos_b', 'rpe2_lw', 'rpe2_lb', 'rpe2_out_w', 'rpe2_out_b')}
    del _L0_conv_all
    return {'x': x, 'L0_conv_u_w': _L0_conv_in['u_w'], 'L0_conv_u_b': _L0_conv_in['u_b'], 'L0_conv_v_w': _L0_conv_in['v_w'], 'L0_conv_v_b': _L0_conv_in['v_b'], 'L0_conv_o_w': _L0_conv_in['o_w'], 'L0_conv_o_b': _L0_conv_in['o_b'], 'L0_conv_rpe1_pos_w': _L0_conv_in['rpe1_pos_w'], 'L0_conv_rpe1_pos_b': _L0_conv_in['rpe1_pos_b'], 'L0_conv_rpe1_lw': _L0_conv_in['rpe1_lw'], 'L0_conv_rpe1_lb': _L0_conv_in['rpe1_lb'], 'L0_conv_rpe1_out_w': _L0_conv_in['rpe1_out_w'], 'L0_conv_rpe1_out_b': _L0_conv_in['rpe1_out_b'], 'L0_conv_rpe2_pos_w': _L0_conv_in['rpe2_pos_w'], 'L0_conv_rpe2_pos_b': _L0_conv_in['rpe2_pos_b'], 'L0_conv_rpe2_lw': _L0_conv_in['rpe2_lw'], 'L0_conv_rpe2_lb': _L0_conv_in['rpe2_lb'], 'L0_conv_rpe2_out_w': _L0_conv_in['rpe2_out_w'], 'L0_conv_rpe2_out_b': _L0_conv_in['rpe2_out_b']}

def reference(x, L0_conv_u_w, L0_conv_u_b, L0_conv_v_w, L0_conv_v_b, L0_conv_o_w, L0_conv_o_b, L0_conv_rpe1_pos_w, L0_conv_rpe1_pos_b, L0_conv_rpe1_lw, L0_conv_rpe1_lb, L0_conv_rpe1_out_w, L0_conv_rpe1_out_b, L0_conv_rpe2_pos_w, L0_conv_rpe2_pos_b, L0_conv_rpe2_lw, L0_conv_rpe2_lb, L0_conv_rpe2_out_w, L0_conv_rpe2_out_b):
    import jax
    import jax.numpy as jnp

    def _L0_conv_ref(x, u_w, u_b, v_w, v_b, o_w, o_b, rpe1_pos_w, rpe1_pos_b, rpe1_lw, rpe1_lb, rpe1_out_w, rpe1_out_b, rpe2_pos_w, rpe2_pos_b, rpe2_lw, rpe2_lb, rpe2_out_w, rpe2_out_b, H, W):
        import jax, jax.numpy as jnp
        import numpy as np
        B, HH, WW, E = (8, 64, 64, 96)
        NH = 8
        D1 = 3 * E // NH * NH
        HD = D1 // NH
        RPE = 256
        LAYERS = 3
        EPS = 1e-08

        def srms(x):
            d = x.shape[-1]
            norm = jnp.linalg.norm(x, axis=-1, keepdims=True)
            return x / (norm * d ** (-0.5) + EPS)

        def rpe_net(idx, pos_w, pos_b, lw, lb, out_w, out_b):
            h = idx @ pos_w.T + pos_b
            for i in range(LAYERS):
                h = jax.nn.relu(srms(h)) @ lw[i].T + lb[i]
            h = jax.nn.relu(srms(h)) @ out_w.T + out_b
            return h.reshape(idx.shape[0], NH, HD).transpose(1, 0, 2)

        def tno(v, axis, pos_w, pos_b, lw, lb, out_w, out_b):
            n = v.shape[axis]
            z = jnp.zeros((1,), jnp.float32)
            p = jnp.arange(1, n, dtype=jnp.float32)
            idx = jnp.concatenate([z, p, z, -p[::-1]]).reshape(-1, 1)
            a = rpe_net(idx, pos_w, pos_b, lw, lb, out_w, out_b)
            ak = a[:, None, :, :] if axis == -2 else a[:, :, None, :]
            y = jnp.fft.rfft(v, 2 * n, axis=axis)
            af = jnp.fft.rfft(ak, 2 * n, axis=axis)
            out = jnp.fft.irfft(af * y, 2 * n, axis=axis)
            return out[..., :n, :] if axis == -2 else out[..., :n, :, :]
        shortcut = x
        xn = srms(x)
        u = jax.nn.silu(xn @ u_w.T + u_b)
        v = jax.nn.silu(xn @ v_w.T + v_b)
        b = v.shape[0]
        v = v.reshape(b, H, W, NH, HD).transpose(0, 3, 1, 2, 4)
        out = tno(v, -3, rpe2_pos_w, rpe2_pos_b, rpe2_lw, rpe2_lb, rpe2_out_w, rpe2_out_b) + tno(v, -2, rpe1_pos_w, rpe1_pos_b, rpe1_lw, rpe1_lb, rpe1_out_w, rpe1_out_b)
        out = out.transpose(0, 2, 3, 1, 4).reshape(b, H, W, NH * HD)
        out = u * out
        return out @ o_w.T + o_b + shortcut

    def _gn(v, G=32, eps=1e-05):
        B_, H_, W_, C_ = v.shape
        g = v.reshape(B_, H_, W_, G, C_ // G)
        m = jnp.mean(g, axis=(1, 2, 4), keepdims=True)
        s = jnp.var(g, axis=(1, 2, 4), keepdims=True)
        return ((g - m) / jnp.sqrt(s + eps)).reshape(v.shape)

    def _ln_c(v, eps=1e-06):
        m = jnp.mean(v, axis=-1, keepdims=True)
        s = jnp.var(v, axis=-1, keepdims=True)
        return (v - m) / jnp.sqrt(s + eps)

    def _ln_t(v, eps=1e-05):
        m = jnp.mean(v, axis=-1, keepdims=True)
        s = jnp.var(v, axis=-1, keepdims=True)
        return (v - m) / jnp.sqrt(s + eps)

    def _to_tokens(v):
        B_, H_, W_, C_ = v.shape
        return v.reshape(B_, H_ * W_, C_)

    def _from_tokens(t, like):
        return t.reshape(like.shape)
    x = _L0_conv_ref(x, L0_conv_u_w, L0_conv_u_b, L0_conv_v_w, L0_conv_v_b, L0_conv_o_w, L0_conv_o_b, L0_conv_rpe1_pos_w, L0_conv_rpe1_pos_b, L0_conv_rpe1_lw, L0_conv_rpe1_lb, L0_conv_rpe1_out_w, L0_conv_rpe1_out_b, L0_conv_rpe2_pos_w, L0_conv_rpe2_pos_b, L0_conv_rpe2_lw, L0_conv_rpe2_lb, L0_conv_rpe2_out_w, L0_conv_rpe2_out_b, 64, 64)
    return x

_drawn_inputs = setup_inputs


def setup_inputs(seed=0):
    import zlib

    import numpy as np

    out = dict(_drawn_inputs(seed))
    spreads = {}
    factors = {'L0_conv_u_w': 4.766,
     'L0_conv_u_b': 8.0,
     'L0_conv_v_w': 6.346,
     'L0_conv_v_b': 8.0,
     'L0_conv_o_w': 4.664,
     'L0_conv_o_b': 100.458,
     'L0_conv_rpe1_pos_w': 8.0,
     'L0_conv_rpe1_pos_b': 8.0,
     'L0_conv_rpe1_lw': 7.778,
     'L0_conv_rpe1_lb': 8.0,
     'L0_conv_rpe1_out_w': 6.69,
     'L0_conv_rpe1_out_b': 8.0,
     'L0_conv_rpe2_pos_w': 8.0,
     'L0_conv_rpe2_pos_b': 8.0,
     'L0_conv_rpe2_lw': 7.816,
     'L0_conv_rpe2_lb': 8.0,
     'L0_conv_rpe2_out_w': 6.11,
     'L0_conv_rpe2_out_b': 8.0}
    for name, (base, spread) in spreads.items():
        noise = np.random.default_rng([zlib.crc32(name.encode()), seed]).standard_normal(out[name].shape)
        drawn = base * np.exp(spread * noise) if base else spread * noise
        out[name] = jnp.asarray(drawn.astype(out[name].dtype))
    for name, factor in factors.items():
        out[name] = (out[name] * factor).astype(out[name].dtype)
    return out
```

```python
import concourse.bass as bass
from concourse import mybir
from contextlib import ExitStack

IMAGES, HEIGHT, WIDTH, E = 8, 64, 64, 96
D = 288
RPE, LAYERS = 256, 3
EPS = 1e-8
TINY = 1e-30
P = 128
NB = 4
STEPS = HEIGHT // 2
HALVES = IMAGES // NB
ALL_STEPS = HALVES * STEPS
KE = E + 1
NCH = D // E
GROUP = 32
GROUPS = D // GROUP
UNIT = 8
GU = GROUP // UNIT
UNITS = D // UNIT
HALF_UNITS = 2 * UNITS
RC = RPE // P
TOK = NB * P
STATS = 8
SPC = ALL_STEPS // STATS
CH = 4
LAG_V, LAG_O = 2, 3


def tno_kernel(nc, x, u_wT, u_b, v_wT, v_b, o_wT, o_b, pos_w, pos_b, lwT, lb, out_wT, out_b, out):
    f32, f32r, i32 = mybir.dt.float32, mybir.dt.float32r, mybir.dt.int32
    ALU, ACT, AX = mybir.AluOpType, mybir.ActivationFunctionType, mybir.AxisListType

    ctx = ExitStack()
    with ctx:
        base = -(-nc.sbuf_base // 32) * 32

        def place(name, shape, offset, dtype=f32):
            return nc.alloc_sbuf_tensor_at(name, shape, dtype, offset=base + offset)

        V_BYTES = STEPS * D * NB * 4
        v = place("v", [P, STEPS, D, NB], 0)
        x_all = place("x_all", [P, STATS, SPC * NB, E], 0)
        x_sq = place("x_sq", [P, 2, SPC * NB, E], STATS * SPC * NB * E * 4)
        late = (STATS + 2) * SPC * NB * E * 4
        w_raw = place("w_raw", [KE, 2, D], late)
        n_ss = place("n_ss", [P, ALL_STEPS * NB], late + 2304)
        n_root = place("n_root", [P, ALL_STEPS * NB], late + 3328)
        n_inv = place("n_inv", [P, ALL_STEPS * NB], late + 4352)
        n_new = place("n_new", [P, ALL_STEPS * NB], late + 5376)
        HB = STEPS * GROUP * NB * 4
        vh = place("vh", [P, 2, STEPS, GROUP, NB], V_BYTES)
        toep = place("toep", [P, GU, UNIT, P], V_BYTES + 2 * HB)
        stage = place("stage", [P, 2, 64 * UNIT], V_BYTES + 2 * HB + 16384)
        region_end = V_BYTES + 2 * HB + 16384 + 4096
        g = place("g", [KE, 2, NCH, TOK], V_BYTES)
        ut = place("ut", [E, NCH, TOK], V_BYTES + 12288)
        ysum = place("ysum", [P, 2, D, NB], V_BYTES + 18432)
        xn_b = place("xn_b", [P, 2, NB, E], V_BYTES + 27648)
        xh = place("xh", [KE, 2, TOK], V_BYTES + 32768, f32r)
        xl = place("xl", [KE, 2, TOK], V_BYTES + 36864, f32r)
        x_a = place("x_a", [P, 2, NB, E], V_BYTES + 40960)
        x_b = place("x_b", [P, CH, NB, E], V_BYTES + 44032)
        r_lw = place("r_lw", [P, 2, LAYERS, RC, RPE], V_BYTES)
        r_ow = place("r_ow", [P, 2, RC, D], V_BYTES + 12288)
        r_pos = place("r_pos", [P, P], V_BYTES + 16896)
        r_ones = place("r_ones", [P, P], V_BYTES + 17408)
        r_h = place("r_h", [P, 2, RC, P], V_BYTES + 17920)
        r_sq = place("r_sq", [P, 2, RC, P], V_BYTES + 19968)
        r_in = place("r_in", [P, 2, RC, P], V_BYTES + 22016)
        r_root = place("r_root", [P, 2, P], V_BYTES + 24064)
        r_inv = place("r_inv", [P, 2, P], V_BYTES + 25088)
        r_new = place("r_new", [P, 2, P], V_BYTES + 26112)
        r_a = place("r_a", [P, 2, D], V_BYTES + 27136)
        r_pw = place("r_pw", [P, 2, 2, RC], V_BYTES + 29440)
        r_lb = place("r_lb", [P, 2, LAYERS, RC], V_BYTES + 29472)
        r_ob = place("r_ob", [1, 2, D], V_BYTES + 29536)
        r_posi = place("r_posi", [P, P], V_BYTES + 31840, i32)
        wv = place("wv", [KE, 2, D], region_end, f32r)
        wu = place("wu", [KE, 2, D], region_end + 2304, f32r)
        wo = place("wo", [KE, NCH, P], region_end + 4608)
        ident = place("ident", [P, P], region_end + 6144)
        rn = place("rn", [P, ALL_STEPS * NB], region_end + 6656)
        assert base + region_end + 7680 <= nc.sbuf_usable_end

        ps = ctx.enter_context(nc.psum_tensor("ps", [P, 8, 512], f32))
        V_BANK = [0, 2]
        U_BANK = [0, 1, 2]
        Y_BANK = [4, 5, 3]
        X_BANK, O_BANK = 6, 7

        v_dram = nc.dram_tensor("v_dram", (HALVES, STEPS, P, D * NB), f32, kind="Internal").ap()
        y_dram = nc.dram_tensor("y_dram", (HALVES, STEPS, P, D * NB), f32, kind="Internal").ap()
        a_dram = nc.dram_tensor("a_dram", (2, UNITS, P, UNIT), f32, kind="Internal").ap()

        def by_column(dram, half):
            return dram[half].rearrange("t (q k w) m -> k (t q) w m", q=2, k=2)

        def sem(name):
            return ctx.enter_context(nc.semaphore(name))

        x_all_loaded = [sem(f"x_all_loaded{k}") for k in range(STATS)]
        weights_loaded, rpe_loaded = sem("weights_loaded"), sem("rpe_loaded")
        zeroed, consts_ready, positions = sem("zeroed"), sem("consts_ready"), sem("positions")
        squared, norms_summed, norms_rooted = sem("squared"), sem("norms_summed"), sem("norms_rooted")
        dve_chain = sem("dve_chain")
        rpe_squared, rpe_summed, rpe_rooted = sem("rpe_squared"), sem("rpe_summed"), sem("rpe_rooted")
        rpe_normed, rpe_layer = sem("rpe_normed"), sem("rpe_layer")
        a_ready, a_stored = sem("a_ready"), sem("a_stored")
        xa_loaded = [sem(f"xa_loaded{k}") for k in range(2)]
        xb_loaded = [sem(f"xb_loaded{k}") for k in range(CH)]
        x_scaled, x_transposed, xh_ready, xl_ready = (
            sem("x_scaled"), sem("x_transposed"), sem("xh_ready"), sem("xl_ready"))
        x_projected = sem("x_projected")
        rows_set = sem("rows_set")
        v_first = sem("v_first")
        v_ready, v_stored = sem("v_ready"), sem("v_stored")
        u_part, u_ready = sem("u_part"), sem("u_ready")
        ysum_loaded = [sem(f"ysum_loaded{k}") for k in range(2)]
        ysum_ready, y_transposed, g_ready = sem("ysum_ready"), sem("y_transposed"), sem("g_ready")
        o_projected, o_ready = sem("o_projected"), sem("o_ready")
        o_stored = [sem(f"o_stored{k}") for k in range(CH)]
        stage_loaded = [sem(f"stage_loaded{k}") for k in range(GU)]
        toep_zeroed, toep_ready = sem("toep_zeroed"), sem("toep_ready")
        vh_loaded = [sem(f"vh_loaded{k}") for k in range(2)]
        conv_done, conv_out, yh_stored = sem("conv_done"), sem("conv_out"), sem("yh_stored")

        def wait(engine, semaphore, count):
            if isinstance(count, int) and count <= 0:
                return
            engine.wait_ge(semaphore, count)

        def xs_a(half, t):
            return t if half == 0 else STEPS + 1 + 2 * t

        def xs_b(half, t):
            return STEPS + 2 * t if half == 0 else 3 * STEPS + t

        def chunks(engine, body):
            body(0, True)
            with engine.Fori(1, STEPS // CH) as c:
                body(c, False)

        def groups(engine, row_block, column_block):
            row_block(0, 0)
            with engine.Fori(0, (GROUPS - 1) // 2) as i:
                for k in range(2):
                    row_block(2 * i + (k + 1), GU + 2 * GU * (2 * i + k))
                    column_block(2 * i + k, k, 2 * GU + 2 * GU * (2 * i + k))
            column_block(GROUPS - 1, (GROUPS - 1) % 2, GU + 2 * GU * (GROUPS - 1))

        block = ctx.enter_context(nc.Block())

        @block.sync
        def _(sp):
            for n in range(2):
                sp.dma_start(r_lw[:, n], lwT[n].rearrange("l (c p) o -> p l c o", p=P)).then_inc(rpe_loaded, 16)
                sp.dma_start(r_ow[:, n], out_wT[n].rearrange("(c p) o -> p c o", p=P)).then_inc(rpe_loaded, 16)
                sp.dma_start(r_ob[0:1, n], out_b[n:n + 1, :]).then_inc(rpe_loaded, 16)
            sp.dma_start(r_pw[:, 0], pos_w).then_inc(rpe_loaded, 16)
            sp.dma_start(r_pw[:, 1], pos_b).then_inc(rpe_loaded, 16)
            sp.dma_start(r_lb[:], lb).then_inc(rpe_loaded, 16)
            for k in range(STATS):
                sp.dma_start(x_all[:, k].rearrange("p (s n) e -> p s (n e)", s=SPC),
                             x[SPC * k:SPC * (k + 1)].rearrange("s p m -> p s m")).then_inc(x_all_loaded[k], 16)
            for n, (w, b) in enumerate(((v_wT, v_b), (u_wT, u_b))):
                sp.dma_start(w_raw[0:E, n], w).then_inc(weights_loaded, 16)
                sp.dma_start(w_raw[E:KE, n], b).then_inc(weights_loaded, 16)
            sp.wait_ge(zeroed, 3)
            sp.dma_start(wo[0:E, :, 0:E], o_wT.rearrange("(k c) e -> c k e", c=E)).then_inc(weights_loaded, 16)
            sp.dma_start(wo[E:KE, 0, 0:E], o_b).then_inc(weights_loaded, 16)
            sp.wait_ge(a_ready, 2)
            for n in range(2):
                sp.dma_start(a_dram[n].rearrange("u k c -> k u c"),
                             r_a[:, n].rearrange("p (u c) -> p u c", c=UNIT)).then_inc(a_stored, 16)

            def load_a(half, t, r):
                wait(sp, x_transposed, xs_a(half, t) - (1 if half == 0 else 3))
                sp.dma_start(x_a[:, r % 2].rearrange("p n e -> p (n e)"),
                             x[bass.ds(STEPS * half + t, 1)].rearrange("s p m -> p (s m)")).then_inc(xa_loaded[r % 2], 16)

            def store_v(half, t):
                sp.wait_ge(v_ready, 2 * (STEPS * half + t) + 2)
                sp.dma_start(v_dram[half, bass.ds(t, 1)].rearrange("s p m -> p (s m)"),
                             v[:, bass.ds(t, 1)].rearrange("p s c n -> p (s c n)")).then_inc(v_stored, 16)

            def load_b(half, t, r, first):
                if half or not first:
                    sp.wait_ge(o_stored[r], 16 * (STEPS // CH) * half + t * 4 - 4 * r)
                sp.dma_start(x_b[:, r].rearrange("p n e -> p (n e)"),
                             x[bass.ds(STEPS * half + t, 1)].rearrange("s p m -> p (s m)")).then_inc(xb_loaded[r], 16)
                wait(sp, y_transposed, NCH * (STEPS * half + t - 1))
                sp.dma_start(ysum[:, r % 2].rearrange("p c n -> p (c n)"),
                             y_dram[half, bass.ds(t, 1)].rearrange("s p m -> p (s m)")).then_inc(ysum_loaded[r % 2], 16)

            def store_out(half, t, r):
                sp.wait_ge(o_ready, STEPS * half + t + 1)
                sp.dma_start(out[bass.ds(STEPS * half + t, 1)].rearrange("s p m -> p (s m)"),
                             x_b[:, r].rearrange("p n e -> p (n e)")).then_inc(o_stored[r], 16)

            def phase_a(c, first):
                for r in range(CH):
                    load_a(0, CH * c + r, r)
                    if not first or r >= LAG_V:
                        store_v(0, CH * c + (r - LAG_V))
            chunks(sp, phase_a)
            for t in range(STEPS - LAG_V, STEPS):
                store_v(0, t)

            def phase_c(half):
                sp.wait_ge(a_stored, 32)
                for k in range(CH if half else 0):
                    sp.wait_ge(o_stored[k], 16 * (STEPS // CH) * half)
                wait(sp, x_projected, (STEPS * 3) * half)

                def load_toep(axis, unit, u, n):
                    e = u % 2
                    wait(sp, toep_ready, 2 * (HALF_UNITS * half + n - GU) + 2)
                    src = a_dram[axis, bass.ds(unit, 1)].rearrange("u k c -> (u k) c")[0:1]
                    runs = bass.AP(src.tensor, src.offset, [[UNIT, 64], [1, 64 * UNIT]])
                    sp.dma_start(stage[64 * e:64 * e + 64, u // 2], runs).then_inc(stage_loaded[u], 16)

                def load_vh(group, slot):
                    for k in range(2):
                        sp.dma_start(vh[64 * k:64 * k + 64, slot].rearrange("p w c n -> p w (c n)"),
                                     by_column(v_dram, half)[k][:, :, bass.ds(group * (GROUP * NB), GROUP * NB)]
                                     ).then_inc(vh_loaded[slot], 16)

                def store_yh(group, slot, n):
                    sp.wait_ge(conv_out, HALF_UNITS * half + n)
                    for k in range(2):
                        sp.dma_start(by_column(y_dram, half)[k][:, :, bass.ds(group * (GROUP * NB), GROUP * NB)],
                                     vh[64 * k:64 * k + 64, slot].rearrange("p w c n -> p w (c n)")
                                     ).then_inc(yh_stored, 16)

                def toeps(axis, group, n):
                    for u in range(GU):
                        load_toep(axis, group * GU + u, u, n + u)

                toeps(0, 0, 0)
                sp.wait_ge(v_stored, 16 * STEPS * (half + 1))
                load_vh(0, 0)
                toeps(0, 1, GU)
                load_vh(1, 1)
                toeps(1, 0, 2 * GU)
                done = 2 * GROUPS * 16 * half

                def later(group, slot):
                    n = GU + 2 * GU * (group - 1)
                    toeps(0, group, n)
                    store_yh(group - 2, slot, n)
                    toeps(1, group - 1, n + GU)
                    sp.wait_ge(yh_stored, done + 32 * (group - 1))
                    load_vh(group, slot)
                later(2, 0)
                with sp.Fori(0, (GROUPS - 3) // 2) as i:
                    for k in range(2):
                        later(2 * i + (3 + k), (3 + k) % 2)
                toeps(1, GROUPS - 1, GU + 2 * GU * (GROUPS - 1))
                store_yh(GROUPS - 2, (GROUPS - 2) % 2, GU + 2 * GU * (GROUPS - 1))
                store_yh(GROUPS - 1, (GROUPS - 1) % 2, HALF_UNITS)
                sp.wait_ge(yh_stored, done + 32 * GROUPS)

            def phase_b(half, with_a):
                def body(c, first):
                    for r in range(CH):
                        t = CH * c + r
                        load_b(half, t, r, first)
                        if with_a:
                            load_a(1, t, r)
                            if not first or r >= LAG_V:
                                store_v(1, CH * c + (r - LAG_V))
                        if not first or r >= LAG_O:
                            store_out(half, CH * c + (r - LAG_O), (r - LAG_O) % CH)
                chunks(sp, body)
                if with_a:
                    for t in range(STEPS - LAG_V, STEPS):
                        store_v(1, t)
                for t in range(STEPS - LAG_O, STEPS):
                    store_out(half, t, t % CH)

            phase_c(0)
            phase_b(0, True)
            phase_c(1)
            phase_b(1, False)
            for r in range(CH):
                sp.wait_ge(o_stored[r], 16 * HALVES * STEPS // CH)

        @block.gpsimd
        def _(pool):
            nc.gpsimd.memset(ident[:], 0.0).then_inc(zeroed, 1)
            nc.gpsimd.memset(r_ones[:], 1.0).then_inc(zeroed, 1)
            nc.gpsimd.memset(wo[:], 0.0).then_inc(zeroed, 1)
            pool.wait_ge(zeroed, 3)
            nc.gpsimd.affine_select(out=ident[:], in_=ident[:], compare_op=ALU.not_equal, fill=1.0, base=0,
                                    pattern=[[-1, P]], channel_multiplier=1).then_inc(consts_ready, 1)
            nc.gpsimd.iota(r_posi[:], pattern=[[-1, P]], base=WIDTH - 1, channel_multiplier=0).then_inc(positions, 1)
            pool.wait_ge(positions, 1)
            nc.gpsimd.tensor_copy(r_pos[:], r_posi[:]).then_inc(positions, 1)

            def scale(half, t, source, target, loaded, count):
                pool.wait_ge(loaded, count)
                factor = rn[:, bass.ds((STEPS * half + t) * NB, NB)].unsqueeze(2).to_broadcast([P, NB, E])
                nc.gpsimd.tensor_tensor(out=target, in0=source, in1=factor, op=ALU.mult).then_inc(x_scaled, 1)

            def scale_a(half, t, c, r):
                scale(half, t, x_a[:, r % 2], x_a[:, r % 2], xa_loaded[r % 2],
                      16 * (STEPS // 2) * half + 32 * c + (16 * (r // 2) + 16))

            def scale_b(half, t, c, r):
                back = xs_b(half, t) - (3 if half == 0 else 1)
                if not (isinstance(t, int) and t < 2):
                    pool.wait_ge(x_transposed, back)
                scale(half, t, x_b[:, r], xn_b[:, r % 2], xb_loaded[r], 16 * (STEPS // CH) * half + 16 * c + 16)

            pool.wait_ge(norms_rooted, 2)

            def phase_a(c, first):
                for r in range(CH):
                    scale_a(0, CH * c + r, c, r)
            chunks(pool, phase_a)

            def phase_b(half, with_a):
                def body(c, first):
                    for r in range(CH):
                        t = CH * c + r
                        scale_b(half, t, c, r)
                        pool.wait_ge(ysum_loaded[r % 2], 16 * (STEPS // 2) * half + 32 * c + (16 * (r // 2) + 16))
                        nc.gpsimd.tensor_tensor(out=ysum[:, r % 2].rearrange("p c n -> p (c n)"),
                                                in0=ysum[:, r % 2].rearrange("p c n -> p (c n)"),
                                                in1=v[:, bass.ds(t, 1)].rearrange("p s c n -> p (s c n)"),
                                                op=ALU.add).then_inc(ysum_ready, 1)
                        if with_a:
                            scale_a(1, t, c, r)
                chunks(pool, body)
            phase_b(0, True)
            phase_b(1, False)

        @block.scalar
        def _(act):
            for layer in range(LAYERS + 1):
                act.wait_ge(rpe_summed, layer + 1)
                nc.scalar.activation(r_root[:], ps[:, 0, 0:2 * P].rearrange("p (n k) -> p n k", n=2), ACT.Sqrt,
                                     scale=1.0 / RPE).then_inc(rpe_rooted, 1)
                for k in range(2 * layer, 2 * layer + 2):
                    act.wait_ge(x_all_loaded[k], 16)
                    wait(act, norms_summed, k - 1)
                    nc.scalar.activation(x_sq[:, k % 2], x_all[:, k], ACT.Square).then_inc(squared, 1)
            act.wait_ge(norms_summed, STATS)
            nc.scalar.activation(n_root[:], n_ss[:], ACT.Sqrt, scale=1.0 / E).then_inc(norms_rooted, 1)

            def high(xs, r):
                act.wait_ge(x_transposed, xs + 1)
                wait(act, x_projected, xs - 1)
                nc.scalar.copy(xh[0:E, r % 2], ps[0:E, X_BANK]).then_inc(xh_ready, 1)

            def silu_v(half, t, xs):
                for q in range(2):
                    if q == 0:
                        act.wait_ge(v_first, STEPS * half + t + 1)
                        if half:
                            act.wait_ge(ysum_ready, t + 1)
                    else:
                        act.wait_ge(x_projected, xs + 1)
                    nc.scalar.activation(
                        v[:, bass.ds(t, 1), :, 2 * q:2 * q + 2].rearrange("p s c n -> p (s c) n"),
                        ps[:, V_BANK[q]:V_BANK[q] + 2, 0:D].rearrange("p n c -> p c n"),
                        ACT.Silu).then_inc(v_ready, 1)

            def silu_u(half, t, xs):
                for k in range(NCH):
                    if k < NCH - 1:
                        act.wait_ge(u_part, (NCH - 1) * (STEPS * half + t) + (k + 1))
                    else:
                        act.wait_ge(x_projected, xs + 1)
                    wait(act, g_ready, NCH * (STEPS * half + t) - (NCH - 1 - k))
                    nc.scalar.activation(ut[:, k], ps[0:E, U_BANK[k]], ACT.Silu).then_inc(u_ready, 1)

            def phase_a(c, first):
                for r in range(CH):
                    t = CH * c + r
                    high(xs_a(0, t), r)
                    silu_v(0, t, xs_a(0, t))
            chunks(act, phase_a)

            def phase_c(half):
                def evacuate(n, u, target):
                    act.wait_ge(conv_done, HALF_UNITS * half + n + 1)
                    nc.scalar.copy(target, ps[:, 2 * u:2 * u + 2].rearrange(
                        "p k (c t n) -> p t (k c) n", c=NB, t=STEPS)).then_inc(conv_out, 1)

                def rows(group, n):
                    for u in range(GU):
                        evacuate(n + u, u, v[:, :, bass.ds(group * GROUP + u * UNIT, UNIT), :])

                def columns(group, slot, n):
                    for u in range(GU):
                        evacuate(n + u, u, vh[:, slot, :, u * UNIT:(u + 1) * UNIT, :])
                groups(act, rows, columns)

            def phase_b(half, with_a):
                def body(c, first):
                    for r in range(CH):
                        t = CH * c + r
                        high(xs_b(half, t), 0 if with_a else r)
                        silu_u(half, t, xs_b(half, t))
                        if with_a:
                            high(xs_a(1, t), 1)
                            silu_v(1, t, xs_a(1, t))
                chunks(act, body)
            phase_c(0)
            phase_b(0, True)
            phase_c(1)
            phase_b(1, False)

        @block.vector
        def _(dve):
            links = [0]

            def link(instruction):
                links[0] += 1
                instruction.then_inc(dve_chain, 1)
                dve.wait_ge(dve_chain, links[0])

            def inverse(target, root, inv, new, total, scale):
                link(nc.vector.tensor_scalar_max(root, root, TINY))
                link(nc.vector.reciprocal(inv, root))
                link(nc.vector.scalar_tensor_tensor(out=new, in0=total, scalar=scale, in1=inv,
                                                    op0=ALU.mult, op1=ALU.mult))
                link(nc.vector.tensor_tensor(out=new, in0=new, in1=root, op=ALU.add))
                link(nc.vector.tensor_scalar(new, new, 0.5, EPS, ALU.mult, ALU.add))
                return nc.vector.reciprocal(target, new)

            def sum_squares(k):
                dve.wait_ge(squared, k + 1)
                nc.vector.reduce_sum(n_ss[:, SPC * NB * k:SPC * NB * (k + 1)], x_sq[:, k % 2],
                                     axis=AX.X).then_inc(norms_summed, 1)

            dve.wait_ge(rpe_loaded, 9 * 16)
            dve.wait_ge(positions, 2)
            for n in range(2):
                for c in range(RC):
                    last = nc.vector.tensor_scalar(r_h[:, n, c], r_pos[:], r_pw[:, 0, n, c:c + 1],
                                                   r_pw[:, 1, n, c:c + 1], ALU.mult, ALU.add)
            link(last)
            for layer in range(LAYERS + 1):
                nc.vector.tensor_tensor(out=r_sq[:], in0=r_h[:], in1=r_h[:], op=ALU.mult).then_inc(rpe_squared, 1)
                for k in range(2 * layer - 2, 2 * layer):
                    if k >= 0:
                        sum_squares(k)
                dve.wait_ge(rpe_rooted, layer + 1)
                link(inverse(r_inv[:], r_root[:], r_inv[:], r_new[:],
                             ps[:, 0, 0:2 * P].rearrange("p (n k) -> p n k", n=2), 1.0 / RPE))
                for c in range(RC):
                    nc.vector.scalar_tensor_tensor(out=r_in[:, :, c], in0=r_h[:, :, c], scalar=0.0, in1=r_inv[:],
                                                   op0=ALU.max, op1=ALU.mult).then_inc(rpe_normed, 1)
                dve.wait_ge(rpe_layer, layer + 1)
                if layer < LAYERS:
                    for n in range(2):
                        for c in range(RC):
                            last = nc.vector.tensor_scalar(
                                r_h[:, n, c], ps[:, 1, (RC * n + c) * P:(RC * n + c + 1) * P],
                                r_lb[:, n, layer, c:c + 1], None, ALU.add)
                    link(last)
                else:
                    for n in range(2):
                        nc.vector.tensor_copy(r_a[:, n], ps[:, 2 + n, 0:D]).then_inc(a_ready, 1)

            for k in range(STATS - 2, STATS):
                sum_squares(k)
            dve.wait_ge(norms_rooted, 1)
            inverse(rn[:], n_root[:], n_inv[:], n_new[:], n_ss[:], 1.0 / E).then_inc(norms_rooted, 1)

            dve.wait_ge(weights_loaded, 6 * 16)
            for n, w in enumerate((wv, wu)):
                link(nc.vector.tensor_copy(w[:, 0], w_raw[:, n]))
                link(nc.vector.tensor_tensor(out=w[:, 1], in0=w_raw[:, n], in1=w[:, 0].bitcast(f32), op=ALU.subtract))

            def bias_rows():
                nc.vector.memset(xh[E:KE].bitcast(f32), 1.0).then_inc(rows_set, 1)
                nc.vector.memset(xl[E:KE].bitcast(f32), 0.0).then_inc(rows_set, 1)

            def low(xs, r):
                dve.wait_ge(xh_ready, xs + 1)
                nc.vector.tensor_tensor(out=xl[0:E, r % 2], in0=ps[0:E, X_BANK], in1=xh[0:E, r % 2].bitcast(f32),
                                        op=ALU.subtract).then_inc(xl_ready, 1)

            bias_rows()

            def phase_a(c, first):
                for r in range(CH):
                    low(xs_a(0, CH * c + r), r)
            chunks(dve, phase_a)

            def phase_c(half):
                dve.wait_ge(x_projected, STEPS if half == 0 else 3 * STEPS)
                for k in range(CH if half else 0):
                    dve.wait_ge(o_stored[k], 16 * STEPS // CH)
                nc.vector.memset(toep[0:64, :, :, 64:P], 0.0).then_inc(toep_zeroed, 1)
                nc.vector.memset(toep[64:P, :, :, 0:64], 0.0).then_inc(toep_zeroed, 1)

                def pair(u, n, count):
                    e = u % 2
                    dve.wait_ge(stage_loaded[u], count)
                    wait(dve, conv_done, HALF_UNITS * half + n - GU + 1)
                    for k in range(2):
                        nc.vector.tensor_copy(toep[64 * k:64 * k + 64, u, :, 64 * k:64 * k + 64],
                                              stage[64 * e:64 * e + 64, u // 2].rearrange("p (i c) -> p c i", c=UNIT)[:, :, ::-1]
                                              ).then_inc(toep_ready, 1)

                def loads(n):
                    return 16 * (2 * GROUPS * half) + (16 // GU) * n + 16

                def rows(group, n):
                    for u in range(GU):
                        pair(u, n + u, loads(n))

                def columns(group, slot, n):
                    for u in range(GU):
                        pair(u, n + u, loads(n))
                groups(dve, rows, columns)

            def phase_b(half, with_a):
                dve.wait_ge(yh_stored, 32 * GROUPS * (half + 1))
                bias_rows()
                nc.vector.memset(g[E:KE, :, 0], 1.0).then_inc(rows_set, 1)

                def body(c, first):
                    for r in range(CH):
                        t = CH * c + r
                        m = STEPS * half + t
                        low(xs_b(half, t), 0 if with_a else r)
                        wait(dve, o_projected, m - 1)
                        for k in range(NCH):
                            dve.wait_ge(u_ready, NCH * m + (k + 1))
                            dve.wait_ge(y_transposed, NCH * m + (k + 1))
                            nc.vector.tensor_tensor(out=g[0:E, r % 2, k], in0=ps[0:E, Y_BANK[k]], in1=ut[:, k],
                                                    op=ALU.mult).then_inc(g_ready, 1)
                        if with_a:
                            low(xs_a(1, t), 1)
                        if not first or r > 0:
                            add_x(m - 1, (r - 1) % CH)
                chunks(dve, body)
                add_x(STEPS * half + STEPS - 1, CH - 1)

            def add_x(m, r):
                dve.wait_ge(o_projected, m + 1)
                nc.vector.tensor_tensor(out=x_b[:, r], in0=ps[:, O_BANK].rearrange("p (n e) -> p n e", n=NB)[:, :, 0:E],
                                        in1=x_b[:, r], op=ALU.add).then_inc(o_ready, 1)

            phase_c(0)
            phase_b(0, True)
            phase_c(1)
            phase_b(1, False)

        @block.tensor
        def _(pe):
            pe.wait_ge(rpe_loaded, 9 * 16)
            pe.wait_ge(zeroed, 3)
            for layer in range(LAYERS + 1):
                pe.wait_ge(rpe_squared, layer + 1)
                for n in range(2):
                    for c in range(RC):
                        last = nc.tensor.matmul(ps[:, 0, n * P:(n + 1) * P], r_ones[:], r_sq[:, n, c],
                                                start=(c == 0), stop=(c == RC - 1))
                last.then_inc(rpe_summed, 1)
                pe.wait_ge(rpe_normed, RC * (layer + 1))
                for n in range(2):
                    if layer < LAYERS:
                        for o in range(RC):
                            for c in range(RC):
                                last = nc.tensor.matmul(ps[:, 1, (RC * n + o) * P:(RC * n + o + 1) * P],
                                                        r_lw[:, n, layer, c, o * P:(o + 1) * P], r_in[:, n, c],
                                                        start=(c == 0), stop=(c == RC - 1))
                    else:
                        for c in range(RC):
                            nc.tensor.matmul(ps[:, 2 + n, 0:D], r_in[:, n, c], r_ow[:, n, c], start=(c == 0), stop=False)
                        last = nc.tensor.matmul(ps[:, 2 + n, 0:D], r_ones[0:1], r_ob[0:1, n], start=False, stop=True)
                last.then_inc(rpe_layer, 1)

            def transpose_x(xs, tile):
                pe.wait_ge(x_scaled, xs + 1)
                wait(pe, xl_ready, xs)
                for n in range(NB):
                    last = nc.tensor.transpose(ps[0:E, X_BANK, n * P:(n + 1) * P], tile[:, n], ident[:])
                last.then_inc(x_transposed, 1)

            SPLIT = ((0, 0), (1, 0), (0, 1))

            def project_v(half, t, xs, r):
                pe.wait_ge(xl_ready, xs + 1)
                if half:
                    m = t + 1
                    pe.wait_ge(u_ready, NCH * m)
                    pe.wait_ge(g_ready, NCH * m)
                for n in range(NB):
                    if n % 2 == 0:
                        wait(pe, v_ready, 2 * (STEPS * half + t) - 1 + n // 2)
                    for k, (xp, wp) in enumerate(SPLIT):
                        last = nc.tensor.matmul(ps[:, V_BANK[n // 2] + n % 2, 0:D], (xh, xl)[xp][:, r % 2, n * P:(n + 1) * P],
                                                wv[:, wp], start=(k == 0), stop=(k == len(SPLIT) - 1))
                    if n % 2:
                        last.then_inc(v_first if n == 1 else x_projected, 1)

            def project_u(half, t, xs, r):
                pe.wait_ge(xl_ready, xs + 1)
                wait(pe, u_ready, NCH * (STEPS * half + t))
                if half == 0:
                    pe.wait_ge(v_ready, 2 * STEPS + 2 * t)
                for k in range(NCH):
                    for s, (xp, wp) in enumerate(SPLIT):
                        last = nc.tensor.matmul(ps[0:E, U_BANK[k]], wu[:, wp, k * E:(k + 1) * E], (xh, xl)[xp][:, r % 2],
                                                start=(s == 0), stop=(s == len(SPLIT) - 1))
                    last.then_inc(u_part if k < NCH - 1 else x_projected, 1)

            def transpose_y(half, t, r):
                m = STEPS * half + t
                pe.wait_ge(ysum_ready, m + 1)
                wait(pe, g_ready, NCH * m)
                for k in range(NCH):
                    if half == 0 and k == NCH - 1:
                        pe.wait_ge(v_ready, 2 * STEPS + 2 * t)
                    for n in range(NB):
                        last = nc.tensor.transpose(ps[0:E, Y_BANK[k], n * P:(n + 1) * P],
                                                   ysum[:, r % 2, k * E:(k + 1) * E, n], ident[:])
                    last.then_inc(y_transposed, 1)

            def project_out(m, r):
                pe.wait_ge(g_ready, NCH * (m + 1))
                wait(pe, o_ready, m)
                for n in range(NB):
                    for k in range(NCH):
                        rows = KE if k == 0 else E
                        last = nc.tensor.matmul(ps[:, O_BANK, n * P:(n + 1) * P], g[0:rows, r % 2, k, n * P:(n + 1) * P],
                                                wo[0:rows, k], start=(k == 0), stop=(k == NCH - 1))
                last.then_inc(o_projected, 1)

            pe.wait_ge(consts_ready, 1)
            pe.wait_ge(rows_set, 2)
            pe.wait_ge(weights_loaded, 6 * 16)

            def phase_a(c, first):
                for r in range(CH):
                    t = CH * c + r
                    transpose_x(xs_a(0, t), x_a[:, r % 2])
                    project_v(0, t, xs_a(0, t), r)
            chunks(pe, phase_a)

            def phase_c(half):
                pe.wait_ge(v_ready, 2 * STEPS * (half + 1))
                if half:
                    pe.wait_ge(o_ready, STEPS)
                pe.wait_ge(toep_zeroed, 2 * (half + 1))

                def unit(n, u, operand):
                    pe.wait_ge(toep_ready, 2 * (HALF_UNITS * half) + 2 * n + 2)
                    wait(pe, conv_out, HALF_UNITS * half + n - GU + 1)
                    for j in range(UNIT):
                        last = nc.tensor.matmul(ps[:, 2 * u + j // NB, (j % NB) * P:(j % NB + 1) * P],
                                                toep[:, u, j], operand(j), start=True, stop=True)
                    last.then_inc(conv_done, 1)

                def rows(group, n):
                    for u in range(GU):
                        unit(n + u, u, lambda j: v[:, :, bass.ds(group * GROUP + (u * UNIT + j), 1), :])

                def columns(group, slot, n):
                    loads = -(-GROUPS // 2) if slot == 0 else GROUPS // 2
                    pe.wait_ge(vh_loaded[slot], 32 * loads * half + 16 * (group - slot) + 32)
                    for u in range(GU):
                        unit(n + u, u, lambda j: vh[:, slot, :, u * UNIT + j, :])
                groups(pe, rows, columns)

            def phase_b(half, with_a):
                pe.wait_ge(conv_out, HALF_UNITS * (half + 1))
                pe.wait_ge(rows_set, 2 + 3 * (half + 1))

                def body(c, first):
                    for r in range(CH):
                        t = CH * c + r
                        m = STEPS * half + t
                        slot = 0 if with_a else r
                        transpose_x(xs_b(half, t), xn_b[:, r % 2])
                        transpose_y(half, t, r)
                        project_u(half, t, xs_b(half, t), slot)
                        if with_a:
                            transpose_x(xs_a(1, t), x_a[:, r % 2])
                        if not first or r > 0:
                            project_out(m - 1, r - 1)
                        if with_a:
                            project_v(1, t, xs_a(1, t), 1)
                chunks(pe, body)
                project_out(STEPS * half + STEPS - 1, CH - 1)

            phase_c(0)
            phase_b(0, True)
            phase_c(1)
            phase_b(1, False)


def kernel(**inputs):
    import numpy as _np
    import concourse.bacc as _bacc
    from concourse import mybir as _mybir
    from concourse.bass_utils import run_bass_kernel_spmd as _run

    get = {k.replace("L0_conv_", ""): _np.asarray(a) for k, a in inputs.items()}
    both = lambda name: _np.stack([get["rpe1_" + name], get["rpe2_" + name]])
    x = get["x"].reshape(HALVES, NB, STEPS, 2, WIDTH, E).transpose(0, 2, 3, 4, 1, 5)
    arrays = {
        "x": x.reshape(ALL_STEPS, P, NB * E),
        "u_wT": get["u_w"].T, "u_b": get["u_b"].reshape(1, D),
        "v_wT": get["v_w"].T, "v_b": get["v_b"].reshape(1, D),
        "o_wT": get["o_w"].T, "o_b": get["o_b"].reshape(1, E),
        "pos_w": both("pos_w").reshape(2, RC, P).transpose(2, 0, 1),
        "pos_b": both("pos_b").reshape(2, RC, P).transpose(2, 0, 1),
        "lwT": both("lw").transpose(0, 1, 3, 2), "lb": both("lb").reshape(2, LAYERS, RC, P).transpose(3, 0, 1, 2),
        "out_wT": both("out_w").transpose(0, 2, 1), "out_b": both("out_b"),
    }
    nc = _bacc.Bacc("TRN2", target_bir_lowering=False, num_devices=1)
    ins, args = {}, []
    for name, a in arrays.items():
        a = _np.ascontiguousarray(a)
        ins[f"in_{name}"] = a
        args.append(nc.dram_tensor(f"in_{name}", a.shape, _mybir.dt.from_np(a.dtype), kind="ExternalInput").ap())
    args.append(nc.dram_tensor("out_0", (ALL_STEPS, P, NB * E), _mybir.dt.float32, kind="ExternalOutput").ap())
    tno_kernel(nc, *args)
    r = _run(nc, [ins], core_ids=[0])
    y = _np.asarray(r.results[0]["out_0"]).reshape(HALVES, STEPS, 2, WIDTH, NB, E)
    return _np.ascontiguousarray(y.transpose(0, 4, 1, 2, 3, 5)).reshape(IMAGES, HEIGHT, WIDTH, E)
```

```python
import concourse.bass as bass
from concourse import mybir
from contextlib import ExitStack

IMAGES, HEIGHT, WIDTH, E = 8, 64, 64, 96
D = 288
RPE, LAYERS = 256, 3
EPS = 1e-8
TINY = 1e-30
P = 128
NB = 4
STEPS = HEIGHT // 2
HALVES = IMAGES // NB
ALL_STEPS = HALVES * STEPS
KE = E + 1
NCH = D // E
GROUP = 32
GROUPS = D // GROUP
UNIT = 8
GU = GROUP // UNIT
UNITS = D // UNIT
HALF_UNITS = 2 * UNITS
RC = RPE // P
TOK = NB * P
CH = 4
NORMS = (CH, 2)
ROOT_GUESS = 0x1FBD1DF5
LAG_V, LAG_O = 2, 3


def tno_kernel(nc, x, u_wT, u_b, v_wT, v_b, o_wT, o_b, pos_w, pos_b, lwT, lb, out_wT, out_b, out):
    f32, f32r, i32 = mybir.dt.float32, mybir.dt.float32r, mybir.dt.int32
    ALU, ACT, AX = mybir.AluOpType, mybir.ActivationFunctionType, mybir.AxisListType

    ctx = ExitStack()
    with ctx:
        base = -(-nc.sbuf_base // 32) * 32

        def place(name, shape, offset, dtype=f32):
            return nc.alloc_sbuf_tensor_at(name, shape, dtype, offset=base + offset)

        V_BYTES = STEPS * D * NB * 4
        v = place("v", [P, STEPS, D, NB], 0)
        w_raw = place("w_raw", [KE, 2, D], 0)
        x_all = place("x_all", [P, STEPS, NB, E], V_BYTES - STEPS * NB * E * 4)
        HB = STEPS * GROUP * NB * 4
        vh = place("vh", [P, 2, STEPS, GROUP, NB], V_BYTES)
        toep = place("toep", [P, GU, UNIT, P], V_BYTES + 2 * HB)
        stage = place("stage", [P, 2, 64 * UNIT], V_BYTES + 2 * HB + 16384)
        region_end = V_BYTES + 2 * HB + 16384 + 4096
        g = place("g", [KE, 2, NCH, TOK], V_BYTES)
        xh = place("xh", [KE, 2, TOK], V_BYTES + 12288, f32r)
        xl = place("xl", [KE, 2, TOK], V_BYTES + 16384, f32r)
        xn_b = place("xn_b", [P, 2, NB, E], V_BYTES + 20480)
        x_a = place("x_a", [P, 2, NB, E], V_BYTES + 23552)
        x_b = place("x_b", [P, CH, NB, E], V_BYTES + 26624)
        ut = place("ut", [E, NCH, TOK], V_BYTES + 32768)
        ysum = place("ysum", [P, 2, D, NB], V_BYTES + 38912)
        x_a0 = place("x_a0", [P, CH, NB, E], V_BYTES + 20480)
        x_sq = place("x_sq", [P, CH * NB, E], V_BYTES + 26624)
        r_lw = place("r_lw", [P, 2, LAYERS, RC, RPE], V_BYTES)
        R = V_BYTES + 32768
        r_ow = place("r_ow", [P, 2, RC, D], R)
        r_pos = place("r_pos", [P, P], R + 4608)
        r_ones = place("r_ones", [P, P], R + 5120)
        r_h = place("r_h", [P, 2, RC, P], R + 5632)
        r_sq = place("r_sq", [P, 2, RC, P], R + 7680)
        r_in = place("r_in", [P, 2, RC, P], R + 9728)
        r_diag = place("r_diag", [P, 2, P], R + 11776)
        r_a = place("r_a", [P, 2, D], R + 12800)
        r_ob = place("r_ob", [1, 2, D], R + 15104)
        r_posi = place("r_posi", [P, P], R + 17408, i32)
        r_pw = place("r_pw", [P, 2, 2, RC], R + 17920)
        r_lb = place("r_lb", [P, 2, LAYERS, RC], R + 17952)
        r_tmp = place("r_tmp", [P, 4, 2], R + 18016)
        wv = place("wv", [KE, 2, D], region_end, f32r)
        wu = place("wu", [KE, 2, D], region_end + 2304, f32r)
        wo = place("wo", [KE, NCH, P], region_end + 4608)
        ident = place("ident", [P, P], region_end + 6144)
        rn = place("rn", [P, ALL_STEPS * NB], region_end + 6656)
        x_n = place("x_n", [P, NORMS[1] * NB, E], region_end + 7680)
        n_tmp = place("n_tmp", [P, 4, CH * NB], region_end + 10752)
        assert base + region_end + 11008 <= nc.sbuf_usable_end

        ps = ctx.enter_context(nc.psum_tensor("ps", [P, 8, 512], f32))
        V_BANK = [0, 2]
        U_BANK = [0, 1, 2]
        Y_BANK = [4, 5, 3]
        X_BANK, O_BANK = 6, 7

        v_dram = nc.dram_tensor("v_dram", (HALVES, STEPS, P, D * NB), f32, kind="Internal").ap()
        y_dram = nc.dram_tensor("y_dram", (HALVES, STEPS, P, D * NB), f32, kind="Internal").ap()
        a_dram = nc.dram_tensor("a_dram", (2, UNITS, P, UNIT), f32, kind="Internal").ap()

        def by_column(dram, half):
            return dram[half].rearrange("t (q k w) m -> k (t q) w m", q=2, k=2)

        def sem(name):
            return ctx.enter_context(nc.semaphore(name))

        x_all_loaded = sem("x_all_loaded")
        weights_loaded, wo_loaded, rpe_loaded = sem("weights_loaded"), sem("wo_loaded"), sem("rpe_loaded")
        zeroed, consts_ready, positions = sem("zeroed"), sem("consts_ready"), sem("positions")
        dve_chain, norm_chain = sem("dve_chain"), sem("norm_chain")
        rpe_squared, rpe_summed, rpe_diag = sem("rpe_squared"), sem("rpe_summed"), sem("rpe_diag")
        rpe_spread, rpe_normed, rpe_layer = sem("rpe_spread"), sem("rpe_normed"), sem("rpe_layer")
        a_ready, a_stored = sem("a_ready"), sem("a_stored")
        xn_loaded, squared, norms_summed, norms_ready = (
            sem("xn_loaded"), sem("squared"), sem("norms_summed"), sem("norms_ready"))
        xa_loaded = [sem(f"xa_loaded{k}") for k in range(2)]
        xb_loaded = [sem(f"xb_loaded{k}") for k in range(CH)]
        x_scaled, x_transposed, xh_ready, xl_ready = (
            sem("x_scaled"), sem("x_transposed"), sem("xh_ready"), sem("xl_ready"))
        x_projected = sem("x_projected")
        rows_set = sem("rows_set")
        v_first = sem("v_first")
        v_ready, v_stored = sem("v_ready"), sem("v_stored")
        u_part, u_ready = sem("u_part"), sem("u_ready")
        ysum_loaded = [sem(f"ysum_loaded{k}") for k in range(2)]
        ysum_ready, y_transposed, g_ready = sem("ysum_ready"), sem("y_transposed"), sem("g_ready")
        o_projected, o_ready = sem("o_projected"), sem("o_ready")
        o_stored = [sem(f"o_stored{k}") for k in range(CH)]
        stage_loaded = [sem(f"stage_loaded{k}") for k in range(GU)]
        toep_zeroed, toep_ready = sem("toep_zeroed"), sem("toep_ready")
        vh_loaded = [sem(f"vh_loaded{k}") for k in range(2)]
        conv_done, conv_out, yh_stored = sem("conv_done"), sem("conv_out"), sem("yh_stored")

        def wait(engine, semaphore, count):
            if isinstance(count, int) and count <= 0:
                return
            engine.wait_ge(semaphore, count)

        def xs_a(half, t):
            return t if half == 0 else STEPS + 1 + 2 * t

        def xs_b(half, t):
            return STEPS + 2 * t if half == 0 else 3 * STEPS + t

        def chunks(engine, body, alone=1, after=None):
            for c in range(alone):
                body(c, c == 0, False)
            if after:
                after()
            with engine.Fori(alone, STEPS // CH - 1) as c:
                body(c, False, False)
            body(STEPS // CH - 1, False, True)

        def groups(engine, row_block, column_block):
            row_block(0, 0)
            with engine.Fori(0, (GROUPS - 1) // 2) as i:
                for k in range(2):
                    row_block(2 * i + (k + 1), GU + 2 * GU * (2 * i + k))
                    column_block(2 * i + k, k, 2 * GU + 2 * GU * (2 * i + k))
            column_block(GROUPS - 1, (GROUPS - 1) % 2, GU + 2 * GU * (GROUPS - 1))

        block = ctx.enter_context(nc.Block())

        @block.sync
        def _(sp):
            def load_x_all(c):
                wait(sp, x_all_loaded, 16 * c)
                sp.dma_start(x_all[:, CH * c:CH * (c + 1)].rearrange("p s n e -> p s (n e)"),
                             x[CH * c:CH * (c + 1)].rearrange("s p m -> p s m")).then_inc(x_all_loaded, 16)

            load_x_all(0)
            sp.dma_start(r_pw[:, 0], pos_w).then_inc(rpe_loaded, 16)
            sp.dma_start(r_pw[:, 1], pos_b).then_inc(rpe_loaded, 16)
            sp.dma_start(w_raw[0:E, 0], v_wT).then_inc(weights_loaded, 16)
            sp.dma_start(w_raw[E:KE, 0], v_b).then_inc(weights_loaded, 16)
            sp.dma_start(w_raw[0:E, 1], u_wT).then_inc(weights_loaded, 16)
            sp.dma_start(w_raw[E:KE, 1], u_b).then_inc(weights_loaded, 16)
            load_x_all(1)
            sp.dma_start(r_lb[:], lb).then_inc(rpe_loaded, 16)
            for n in range(2):
                sp.dma_start(r_lw[:, n], lwT[n].rearrange("l (c p) o -> p l c o", p=P)).then_inc(rpe_loaded, 16)
                sp.dma_start(r_ow[:, n], out_wT[n].rearrange("(c p) o -> p c o", p=P)).then_inc(rpe_loaded, 16)
                sp.dma_start(r_ob[0:1, n], out_b[n:n + 1, :]).then_inc(rpe_loaded, 16)
            for c in range(2, STEPS // CH):
                load_x_all(c)
            sp.wait_ge(zeroed, 3)
            sp.dma_start(wo[0:E, :, 0:E], o_wT.rearrange("(k c) e -> c k e", c=E)).then_inc(wo_loaded, 16)
            sp.dma_start(wo[E:KE, 0, 0:E], o_b).then_inc(wo_loaded, 16)

            def store_a():
                sp.wait_ge(a_ready, 2)
                for n in range(2):
                    sp.dma_start(a_dram[n].rearrange("u k c -> k u c"),
                                 r_a[:, n].rearrange("p (u c) -> p u c", c=UNIT)).then_inc(a_stored, 16)

            def load_a(t, r):
                sp.wait_ge(x_transposed, xs_a(1, t) - 3)
                sp.dma_start(x_a[:, r % 2].rearrange("p n e -> p (n e)"),
                             x[bass.ds(STEPS + t, 1)].rearrange("s p m -> p (s m)")).then_inc(xa_loaded[r % 2], 16)

            def load_norms(j):
                wait(sp, norms_summed, STEPS // NORMS[0] + j)
                sp.dma_start(x_n[:].rearrange("p (s n) e -> p s (n e)", n=NB),
                             x[bass.ds(STEPS + NORMS[1] * j, NORMS[1])].rearrange("s p m -> p s m")
                             ).then_inc(xn_loaded, 16)

            def store_v(half, t):
                sp.wait_ge(v_ready, 2 * (STEPS * half + t) + 2)
                sp.dma_start(v_dram[half, bass.ds(t, 1)].rearrange("s p m -> p (s m)"),
                             v[:, bass.ds(t, 1)].rearrange("p s c n -> p (s c n)")).then_inc(v_stored, 16)

            def load_b(half, t, r, first):
                if half or not first:
                    sp.wait_ge(o_stored[r], 16 * (STEPS // CH) * half + t * 4 - 4 * r)
                sp.dma_start(x_b[:, r].rearrange("p n e -> p (n e)"),
                             x[bass.ds(STEPS * half + t, 1)].rearrange("s p m -> p (s m)")).then_inc(xb_loaded[r], 16)
                wait(sp, y_transposed, NCH * (STEPS * half + t - 1))
                sp.dma_start(ysum[:, r % 2].rearrange("p c n -> p (c n)"),
                             y_dram[half, bass.ds(t, 1)].rearrange("s p m -> p (s m)")).then_inc(ysum_loaded[r % 2], 16)

            def store_out(half, t, r):
                sp.wait_ge(o_ready, STEPS * half + t + 1)
                sp.dma_start(out[bass.ds(STEPS * half + t, 1)].rearrange("s p m -> p (s m)"),
                             x_b[:, r].rearrange("p n e -> p (n e)")).then_inc(o_stored[r], 16)

            def phase_a(c, first, last):
                for r in range(CH):
                    store_v(0, CH * c + r)
            chunks(sp, phase_a, LAYERS + 1, store_a)
            load_norms(0)

            def phase_c(half):
                sp.wait_ge(a_stored, 32)
                for k in range(CH if half else 0):
                    sp.wait_ge(o_stored[k], 16 * (STEPS // CH) * half)
                wait(sp, x_projected, (STEPS * 3) * half)

                def load_toep(axis, unit, u, n):
                    e = u % 2
                    wait(sp, toep_ready, 2 * (HALF_UNITS * half + n - GU) + 2)
                    src = a_dram[axis, bass.ds(unit, 1)].rearrange("u k c -> (u k) c")[0:1]
                    runs = bass.AP(src.tensor, src.offset, [[UNIT, 64], [1, 64 * UNIT]])
                    sp.dma_start(stage[64 * e:64 * e + 64, u // 2], runs).then_inc(stage_loaded[u], 16)

                def load_vh(group, slot):
                    for k in range(2):
                        sp.dma_start(vh[64 * k:64 * k + 64, slot].rearrange("p w c n -> p w (c n)"),
                                     by_column(v_dram, half)[k][:, :, bass.ds(group * (GROUP * NB), GROUP * NB)]
                                     ).then_inc(vh_loaded[slot], 16)

                def store_yh(group, slot, n):
                    sp.wait_ge(conv_out, HALF_UNITS * half + n)
                    for k in range(2):
                        sp.dma_start(by_column(y_dram, half)[k][:, :, bass.ds(group * (GROUP * NB), GROUP * NB)],
                                     vh[64 * k:64 * k + 64, slot].rearrange("p w c n -> p w (c n)")
                                     ).then_inc(yh_stored, 16)

                def toeps(axis, group, n):
                    for u in range(GU):
                        load_toep(axis, group * GU + u, u, n + u)

                toeps(0, 0, 0)
                sp.wait_ge(v_stored, 16 * STEPS * (half + 1))
                load_vh(0, 0)
                toeps(0, 1, GU)
                load_vh(1, 1)
                toeps(1, 0, 2 * GU)
                toeps(0, 2, 3 * GU)
                done = 2 * GROUPS * 16 * half

                def later(group, slot, last=False):
                    n = GU + 2 * GU * (group - 1)
                    toeps(1, group - 1, n + GU)
                    store_yh(group - 2, slot, n)
                    if not last:
                        toeps(0, group + 1, n + 2 * GU)
                    sp.wait_ge(yh_stored, done + 32 * (group - 1))
                    load_vh(group, slot)
                with sp.Fori(0, (GROUPS - 3) // 2) as i:
                    for k in range(2):
                        later(2 * i + (2 + k), k)
                later(GROUPS - 1, (GROUPS - 1) % 2, True)
                toeps(1, GROUPS - 1, GU + 2 * GU * (GROUPS - 1))
                store_yh(GROUPS - 2, (GROUPS - 2) % 2, GU + 2 * GU * (GROUPS - 1))
                store_yh(GROUPS - 1, (GROUPS - 1) % 2, HALF_UNITS)
                sp.wait_ge(yh_stored, done + 32 * GROUPS)

            def phase_b(half, with_a):
                def body(c, first, last):
                    for r in range(CH):
                        t = CH * c + r
                        load_b(half, t, r, first)
                        if with_a:
                            load_a(t, r)
                            if r % 2 == 0 and not (last and r == CH - 2):
                                load_norms(2 * c + (r // 2 + 1))
                            if not first or r >= LAG_V:
                                store_v(1, CH * c + (r - LAG_V))
                        if not first or r >= LAG_O:
                            store_out(half, CH * c + (r - LAG_O), (r - LAG_O) % CH)
                chunks(sp, body)
                if with_a:
                    for t in range(STEPS - LAG_V, STEPS):
                        store_v(1, t)
                for t in range(STEPS - LAG_O, STEPS):
                    store_out(half, t, t % CH)

            phase_c(0)
            phase_b(0, True)
            phase_c(1)
            phase_b(1, False)
            for r in range(CH):
                sp.wait_ge(o_stored[r], 16 * HALVES * STEPS // CH)

        @block.gpsimd
        def _(pool):
            nc.gpsimd.memset(ident[:], 0.0).then_inc(zeroed, 1)
            nc.gpsimd.memset(r_ones[:], 1.0).then_inc(zeroed, 1)
            nc.gpsimd.memset(wo[:], 0.0).then_inc(zeroed, 1)
            pool.wait_ge(zeroed, 3)
            nc.gpsimd.affine_select(out=ident[:], in_=ident[:], compare_op=ALU.not_equal, fill=1.0, base=0,
                                    pattern=[[-1, P]], channel_multiplier=1).then_inc(consts_ready, 1)
            nc.gpsimd.iota(r_posi[:], pattern=[[-1, P]], base=WIDTH - 1, channel_multiplier=0).then_inc(positions, 1)
            pool.wait_ge(positions, 1)
            nc.gpsimd.tensor_copy(r_pos[:], r_posi[:]).then_inc(positions, 1)

            def scale(half, t, source, target):
                factor = rn[:, bass.ds((STEPS * half + t) * NB, NB)].unsqueeze(2).to_broadcast([P, NB, E])
                nc.gpsimd.tensor_tensor(out=target, in0=source, in1=factor, op=ALU.mult).then_inc(x_scaled, 1)

            def scale_a0(t, c, r):
                pool.wait_ge(norms_ready, c + 1)
                wait(pool, x_transposed, t - (CH - 1))
                scale(0, t, x_all[:, bass.ds(t, 1)].rearrange("p s n e -> p (s n) e"), x_a0[:, r])

            def scale_a1(t, c, r):
                pool.wait_ge(norms_ready, STEPS // NORMS[0] + 2 * c + (r // 2 + 1))
                pool.wait_ge(xa_loaded[r % 2], 32 * c + (16 * (r // 2) + 16))
                scale(1, t, x_a[:, r % 2], x_a[:, r % 2])

            def square(source, target):
                nc.gpsimd.tensor_tensor(out=target, in0=source, in1=source, op=ALU.mult).then_inc(squared, 1)

            def square_a0(c, r):
                if r == 0:
                    pool.wait_ge(x_all_loaded, 16 * (c + 1))
                    wait(pool, norms_summed, c)
                square(x_all[:, bass.ds(CH * c + r, 1)].rearrange("p s n e -> p (s n) e"),
                       x_sq[:, NB * r:NB * (r + 1)])

            def square_a1(j):
                pool.wait_ge(xn_loaded, 16 * (j + 1))
                square(x_n[:], x_n[:])

            def scale_b(half, t, c, r):
                back = xs_b(half, t) - (3 if half == 0 else 1)
                if not (isinstance(t, int) and t < 2):
                    pool.wait_ge(x_transposed, back)
                pool.wait_ge(xb_loaded[r], 16 * (STEPS // CH) * half + 16 * c + 16)
                scale(half, t, x_b[:, r], xn_b[:, r % 2])

            for r in range(CH):
                square_a0(0, r)

            def phase_a(c, first, last):
                for r in range(CH):
                    scale_a0(CH * c + r, c, r)
                    if not last:
                        square_a0(c + 1, r)
            chunks(pool, phase_a)
            square_a1(0)

            def zero_toep(half):
                for k in range(2):
                    nc.gpsimd.memset(toep[64 * k:64 * k + 64, :, :, 64 - 64 * k:P - 64 * k], 0.0).then_inc(toep_zeroed, 1)
                    pool.wait_ge(toep_zeroed, 2 * half + k + 1)

            pool.wait_ge(a_stored, 32)
            pool.wait_ge(squared, CH * (STEPS // CH) + 1)
            zero_toep(0)

            def phase_b(half, with_a):
                scale_b(half, 0, 0, 0)

                def body(c, first, last):
                    for r in range(CH):
                        t = CH * c + r
                        pool.wait_ge(ysum_loaded[r % 2], 16 * (STEPS // 2) * half + 32 * c + (16 * (r // 2) + 16))
                        nc.gpsimd.tensor_tensor(out=ysum[:, r % 2].rearrange("p c n -> p (c n)"),
                                                in0=ysum[:, r % 2].rearrange("p c n -> p (c n)"),
                                                in1=v[:, bass.ds(t, 1)].rearrange("p s c n -> p (s c n)"),
                                                op=ALU.add).then_inc(ysum_ready, 1)
                        if with_a:
                            if r % 2 == 0 and not (last and r == CH - 2):
                                square_a1(2 * c + (r // 2 + 1))
                            scale_a1(t, c, r)
                        if r < CH - 1:
                            scale_b(half, t + 1, c, r + 1)
                        elif not last:
                            scale_b(half, t + 1, c + 1, 0)
                chunks(pool, body)
            phase_b(0, True)
            pool.wait_ge(g_ready, NCH * STEPS)
            pool.wait_ge(x_scaled, 3 * STEPS)
            zero_toep(1)
            phase_b(1, False)

        @block.scalar
        def _(act):
            def high(xs, r):
                act.wait_ge(x_transposed, xs + 1)
                wait(act, x_projected, xs - 1)
                nc.scalar.copy(xh[0:E, r % 2], ps[0:E, X_BANK]).then_inc(xh_ready, 1)

            def silu_v(half, t, xs):
                for q in range(2):
                    if q == 0:
                        act.wait_ge(v_first, STEPS * half + t + 1)
                        if half:
                            act.wait_ge(ysum_ready, t + 1)
                    else:
                        act.wait_ge(x_projected, xs + 1)
                    nc.scalar.activation(
                        v[:, bass.ds(t, 1), :, 2 * q:2 * q + 2].rearrange("p s c n -> p (s c) n"),
                        ps[:, V_BANK[q]:V_BANK[q] + 2, 0:D].rearrange("p n c -> p c n"),
                        ACT.Silu).then_inc(v_ready, 1)

            def silu_u(half, t, xs):
                for k in range(NCH):
                    if k < NCH - 1:
                        act.wait_ge(u_part, (NCH - 1) * (STEPS * half + t) + (k + 1))
                    else:
                        act.wait_ge(x_projected, xs + 1)
                    wait(act, g_ready, NCH * (STEPS * half + t) - (NCH - 1 - k))
                    nc.scalar.activation(ut[:, k], ps[0:E, U_BANK[k]], ACT.Silu).then_inc(u_ready, 1)

            high(xs_a(0, 0), 0)

            def phase_a(c, first, last):
                for r in range(CH):
                    t = CH * c + r
                    if not (last and r == CH - 1):
                        high(xs_a(0, t + 1), r + 1)
                    silu_v(0, t, xs_a(0, t))
            chunks(act, phase_a)

            def phase_c(half):
                def evacuate(n, u, target):
                    act.wait_ge(conv_done, HALF_UNITS * half + n + 1)
                    nc.scalar.copy(target, ps[:, 2 * u:2 * u + 2].rearrange(
                        "p k (c t n) -> p t (k c) n", c=NB, t=STEPS)).then_inc(conv_out, 1)

                def rows(group, n):
                    for u in range(GU):
                        evacuate(n + u, u, v[:, :, bass.ds(group * GROUP + u * UNIT, UNIT), :])

                def columns(group, slot, n):
                    for u in range(GU):
                        evacuate(n + u, u, vh[:, slot, :, u * UNIT:(u + 1) * UNIT, :])
                groups(act, rows, columns)

            def phase_b(half, with_a):
                high(xs_b(half, 0), 0)

                def body(c, first, last):
                    for r in range(CH):
                        t = CH * c + r
                        more = not (last and r == CH - 1)
                        if with_a:
                            high(xs_a(1, t), 1)
                            silu_u(half, t, xs_b(half, t))
                            if more:
                                high(xs_b(half, t + 1), 0)
                            silu_v(1, t, xs_a(1, t))
                        else:
                            if more:
                                high(xs_b(half, t + 1), r + 1)
                            silu_u(half, t, xs_b(half, t))
                chunks(act, body)
            phase_c(0)
            phase_b(0, True)
            phase_c(1)
            phase_b(1, False)

        @block.vector
        def _(dve):
            links = [0]

            def link(instruction):
                links[0] += 1
                instruction.then_inc(dve_chain, 1)
                dve.wait_ge(dve_chain, links[0])

            def inverse(target, total, root, inv, source, scale):
                ts = nc.vector.tensor_scalar
                steps = [lambda: ts(total, source, scale, None, ALU.mult),
                         lambda: ts(root.bitcast(i32), total.bitcast(i32), 1, None, ALU.logical_shift_right),
                         lambda: ts(root.bitcast(i32), root.bitcast(i32), float(ROOT_GUESS), None, ALU.add),
                         lambda: ts(root, root, 2.0, None, ALU.mult),
                         lambda: ts(total, total, 2.0, None, ALU.mult)]
                for _ in range(3):
                    steps += [lambda: nc.vector.reciprocal(inv, root),
                              lambda: nc.vector.tensor_tensor(out=inv, in0=inv, in1=total, op=ALU.mult),
                              lambda: nc.vector.scalar_tensor_tensor(out=root, in0=root, scalar=0.5, in1=inv,
                                                                     op0=ALU.mult, op1=ALU.add)]
                return steps + [lambda: ts(root, root, 0.5, EPS, ALU.mult, ALU.add),
                                lambda: nc.vector.reciprocal(target, root)]

            dve.wait_ge(weights_loaded, 4 * 16)
            for n, w in enumerate((wv, wu)):
                link(nc.vector.tensor_copy(w[:, 0], w_raw[:, n]))
                link(nc.vector.tensor_tensor(out=w[:, 1], in0=w_raw[:, n], in1=w[:, 0].bitcast(f32), op=ALU.subtract))

            def bias_rows():
                nc.vector.memset(xh[E:KE].bitcast(f32), 1.0).then_inc(rows_set, 1)
                nc.vector.memset(xl[E:KE].bitcast(f32), 0.0).then_inc(rows_set, 1)

            def norms(parts, first_step, steps, x2, batch):
                cols = steps * NB
                total, root, inv = (n_tmp[:, k, 0:cols] for k in range(3))
                small = inverse(rn[:, bass.ds(first_step * NB, cols)], total, root, inv, total, 1.0 / E)
                for part in parts:
                    if part == 0:
                        dve.wait_ge(squared, CH * (batch + 1) if steps == CH else batch + (CH - 1) * (STEPS // CH) + 1)
                        nc.vector.reduce_sum(total, x2, axis=AX.X).then_inc(norms_summed, 1)
                        dve.wait_ge(norms_summed, batch + 1)
                        continue
                    half_way = len(small) // 2
                    for k in range(half_way * (part - 1), half_way * part):
                        if k < len(small) - 1:
                            small[k]().then_inc(norm_chain, 1)
                            dve.wait_ge(norm_chain, (len(small) - 1) * batch + (k + 1))
                        else:
                            small[k]().then_inc(norms_ready, 1)

            def rpe_part(layer, r):
                if r == 0:
                    nc.vector.tensor_tensor(out=r_sq[:], in0=r_h[:], in1=r_h[:], op=ALU.mult).then_inc(rpe_squared, 1)
                elif r == 1:
                    dve.wait_ge(rpe_summed, layer + 1)
                    for step in inverse(r_tmp[:, 3], r_tmp[:, 0], r_tmp[:, 1], r_tmp[:, 2],
                                        ps[:, 7, 0:2 * P:P], 1.0 / RPE):
                        link(step())
                    for n in range(2):
                        nc.vector.tensor_scalar(r_diag[:, n], ident[:], r_tmp[:, 3, n:n + 1], None,
                                                ALU.mult).then_inc(rpe_diag, 1)
                elif r == 2:
                    dve.wait_ge(rpe_spread, layer + 1)
                    for c in range(RC):
                        nc.vector.scalar_tensor_tensor(out=r_in[:, :, c], in0=r_h[:, :, c], scalar=0.0,
                                                       in1=ps[:, 4, 0:2 * P].rearrange("p (n k) -> p n k", n=2),
                                                       op0=ALU.max, op1=ALU.mult).then_inc(rpe_normed, 1)
                else:
                    dve.wait_ge(rpe_layer, layer + 1)
                    for n in range(2):
                        if layer == LAYERS:
                            nc.vector.tensor_copy(r_a[:, n], ps[:, 4 + n, 0:D]).then_inc(a_ready, 1)
                        else:
                            for c in range(RC):
                                last = nc.vector.tensor_scalar(
                                    r_h[:, n, c], ps[:, 5, (RC * n + c) * P:(RC * n + c + 1) * P],
                                    r_lb[:, n, layer, c:c + 1], None, ALU.add)
                    if layer < LAYERS:
                        link(last)

            def low(xs, r):
                dve.wait_ge(xh_ready, xs + 1)
                nc.vector.tensor_tensor(out=xl[0:E, r % 2], in0=ps[0:E, X_BANK], in1=xh[0:E, r % 2].bitcast(f32),
                                        op=ALU.subtract).then_inc(xl_ready, 1)

            bias_rows()

            norms((0, 1, 2), 0, CH, x_sq[:], 0)
            dve.wait_ge(rpe_loaded, 9 * 16)
            dve.wait_ge(positions, 2)
            for n in range(2):
                for c in range(RC):
                    last = nc.vector.tensor_scalar(r_h[:, n, c], r_pos[:], r_pw[:, 0, n, c:c + 1],
                                                   r_pw[:, 1, n, c:c + 1], ALU.mult, ALU.add)
            link(last)
            low(xs_a(0, 0), 0)

            def phase_a(c, first, last):
                for r in range(CH):
                    if not (last and r == CH - 1):
                        low(xs_a(0, CH * c + (r + 1)), r + 1)
                    if not last:
                        norms(((0,), (1,), (2,), ())[r], CH * (c + 1), CH, x_sq[:], c + 1)
                    if isinstance(c, int) and c <= LAYERS:
                        rpe_part(c, r)
            chunks(dve, phase_a, LAYERS + 1)

            def phase_c(half):
                def pair(u, n, count):
                    e = u % 2
                    dve.wait_ge(stage_loaded[u], count)
                    wait(dve, conv_done, HALF_UNITS * half + n - GU + 1)
                    for k in range(2):
                        nc.vector.tensor_copy(toep[64 * k:64 * k + 64, u, :, 64 * k:64 * k + 64],
                                              stage[64 * e:64 * e + 64, u // 2].rearrange("p (i c) -> p c i", c=UNIT)[:, :, ::-1]
                                              ).then_inc(toep_ready, 1)

                def loads(n):
                    return 16 * (2 * GROUPS * half) + (16 // GU) * n + 16

                def rows(group, n):
                    for u in range(GU):
                        pair(u, n + u, loads(n))

                def columns(group, slot, n):
                    for u in range(GU):
                        pair(u, n + u, loads(n))
                groups(dve, rows, columns)

            def phase_b(half, with_a):
                dve.wait_ge(yh_stored, 32 * GROUPS * (half + 1))
                bias_rows()
                nc.vector.memset(g[E:KE, :, 0], 1.0).then_inc(rows_set, 1)

                low(xs_b(half, 0), 0)

                def body(c, first, last):
                    for r in range(CH):
                        t = CH * c + r
                        m = STEPS * half + t
                        more = not (last and r == CH - 1)
                        if with_a:
                            low(xs_a(1, t), 1)
                        elif more:
                            low(xs_b(half, t + 1), r + 1)
                        wait(dve, o_projected, m - 1)
                        for k in range(NCH):
                            dve.wait_ge(u_ready, NCH * m + (k + 1))
                            dve.wait_ge(y_transposed, NCH * m + (k + 1))
                            nc.vector.tensor_tensor(out=g[0:E, r % 2, k], in0=ps[0:E, Y_BANK[k]], in1=ut[:, k],
                                                    op=ALU.mult).then_inc(g_ready, 1)
                        if not first or r > 0:
                            add_x(m - 1, (r - 1) % CH)
                        if with_a:
                            if more:
                                low(xs_b(half, t + 1), 0)
                            if not (last and r >= CH - 2):
                                j = 2 * c + (r // 2 + 1)
                                norms(((0, 1), (2,))[r % 2], STEPS + 2 * j, NORMS[1], x_n[:], STEPS // NORMS[0] + j)
                chunks(dve, body)
                add_x(STEPS * half + STEPS - 1, CH - 1)

            def add_x(m, r):
                dve.wait_ge(o_projected, m + 1)
                nc.vector.tensor_tensor(out=x_b[:, r], in0=ps[:, O_BANK].rearrange("p (n e) -> p n e", n=NB)[:, :, 0:E],
                                        in1=x_b[:, r], op=ALU.add).then_inc(o_ready, 1)

            phase_c(0)
            norms((0, 1, 2), STEPS, NORMS[1], x_n[:], STEPS // NORMS[0])
            phase_b(0, True)
            phase_c(1)
            phase_b(1, False)

        @block.tensor
        def _(pe):
            def rpe_part(layer, r):
                if r == 0:
                    if layer == 0:
                        pe.wait_ge(rpe_loaded, 9 * 16)
                        pe.wait_ge(zeroed, 3)
                    pe.wait_ge(rpe_squared, layer + 1)
                    for n in range(2):
                        for c in range(RC):
                            last = nc.tensor.matmul(ps[:, 7, n * P:(n + 1) * P], r_sq[:, n, c], r_ones[:],
                                                    start=(c == 0), stop=(c == RC - 1))
                    last.then_inc(rpe_summed, 1)
                elif r == 1:
                    pe.wait_ge(rpe_diag, 2 * (layer + 1))
                    for n in range(2):
                        last = nc.tensor.matmul(ps[:, 4, n * P:(n + 1) * P], r_ones[:], r_diag[:, n],
                                                start=True, stop=True)
                    last.then_inc(rpe_spread, 1)
                elif r == 2:
                    pe.wait_ge(rpe_normed, RC * (layer + 1))
                    for n in range(2):
                        if layer < LAYERS:
                            for o in range(RC):
                                for c in range(RC):
                                    last = nc.tensor.matmul(ps[:, 5, (RC * n + o) * P:(RC * n + o + 1) * P],
                                                            r_lw[:, n, layer, c, o * P:(o + 1) * P], r_in[:, n, c],
                                                            start=(c == 0), stop=(c == RC - 1))
                        else:
                            for c in range(RC):
                                nc.tensor.matmul(ps[:, 4 + n, 0:D], r_in[:, n, c], r_ow[:, n, c],
                                                 start=(c == 0), stop=False)
                            last = nc.tensor.matmul(ps[:, 4 + n, 0:D], r_ones[0:1], r_ob[0:1, n], start=False, stop=True)
                    last.then_inc(rpe_layer, 1)

            def transpose_x(xs, tile):
                pe.wait_ge(x_scaled, xs + 1)
                wait(pe, xl_ready, xs)
                for n in range(NB):
                    last = nc.tensor.transpose(ps[0:E, X_BANK, n * P:(n + 1) * P], tile[:, n], ident[:])
                last.then_inc(x_transposed, 1)

            SPLIT = ((0, 0), (1, 0), (0, 1))

            def project_v(half, t, xs, r):
                pe.wait_ge(xl_ready, xs + 1)
                if half:
                    m = t + 1
                    pe.wait_ge(u_ready, NCH * m)
                    pe.wait_ge(g_ready, NCH * m)
                for n in range(NB):
                    if n % 2 == 0:
                        wait(pe, v_ready, 2 * (STEPS * half + t) - 1 + n // 2)
                    for k, (xp, wp) in enumerate(SPLIT):
                        last = nc.tensor.matmul(ps[:, V_BANK[n // 2] + n % 2, 0:D], (xh, xl)[xp][:, r % 2, n * P:(n + 1) * P],
                                                wv[:, wp], start=(k == 0), stop=(k == len(SPLIT) - 1))
                    if n % 2:
                        last.then_inc(v_first if n == 1 else x_projected, 1)

            def project_u(half, t, xs, r):
                pe.wait_ge(xl_ready, xs + 1)
                wait(pe, u_ready, NCH * (STEPS * half + t))
                if half == 0:
                    pe.wait_ge(v_ready, 2 * STEPS + 2 * t)
                for k in range(NCH):
                    for s, (xp, wp) in enumerate(SPLIT):
                        last = nc.tensor.matmul(ps[0:E, U_BANK[k]], wu[:, wp, k * E:(k + 1) * E], (xh, xl)[xp][:, r % 2],
                                                start=(s == 0), stop=(s == len(SPLIT) - 1))
                    last.then_inc(u_part if k < NCH - 1 else x_projected, 1)

            def transpose_y(half, t, r):
                m = STEPS * half + t
                pe.wait_ge(ysum_ready, m + 1)
                wait(pe, g_ready, NCH * m)
                for k in range(NCH):
                    if half == 0 and k == NCH - 1:
                        pe.wait_ge(v_ready, 2 * STEPS + 2 * t)
                    for n in range(NB):
                        last = nc.tensor.transpose(ps[0:E, Y_BANK[k], n * P:(n + 1) * P],
                                                   ysum[:, r % 2, k * E:(k + 1) * E, n], ident[:])
                    last.then_inc(y_transposed, 1)

            def project_out(m, r):
                pe.wait_ge(g_ready, NCH * (m + 1))
                wait(pe, o_ready, m)
                for n in range(NB):
                    for k in range(NCH):
                        rows = KE if k == 0 else E
                        last = nc.tensor.matmul(ps[:, O_BANK, n * P:(n + 1) * P], g[0:rows, r % 2, k, n * P:(n + 1) * P],
                                                wo[0:rows, k], start=(k == 0), stop=(k == NCH - 1))
                last.then_inc(o_projected, 1)

            pe.wait_ge(consts_ready, 1)
            pe.wait_ge(rows_set, 2)

            transpose_x(xs_a(0, 0), x_a0[:, 0])

            def phase_a(c, first, last):
                for r in range(CH):
                    t = CH * c + r
                    if not (last and r == CH - 1):
                        transpose_x(xs_a(0, t + 1), x_a0[:, (r + 1) % CH])
                    project_v(0, t, xs_a(0, t), r)
                    if isinstance(c, int) and c <= LAYERS:
                        rpe_part(c, r)
            chunks(pe, phase_a, LAYERS + 1)

            def phase_c(half):
                pe.wait_ge(v_ready, 2 * STEPS * (half + 1))
                if half:
                    pe.wait_ge(o_ready, STEPS)
                pe.wait_ge(toep_zeroed, 2 * (half + 1))

                def unit(n, u, operand):
                    pe.wait_ge(toep_ready, 2 * (HALF_UNITS * half) + 2 * n + 2)
                    wait(pe, conv_out, HALF_UNITS * half + n - GU + 1)
                    for j in range(UNIT):
                        last = nc.tensor.matmul(ps[:, 2 * u + j // NB, (j % NB) * P:(j % NB + 1) * P],
                                                toep[:, u, j], operand(j), start=True, stop=True)
                    last.then_inc(conv_done, 1)

                def rows(group, n):
                    for u in range(GU):
                        unit(n + u, u, lambda j: v[:, :, bass.ds(group * GROUP + (u * UNIT + j), 1), :])

                def columns(group, slot, n):
                    loads = -(-GROUPS // 2) if slot == 0 else GROUPS // 2
                    pe.wait_ge(vh_loaded[slot], 32 * loads * half + 16 * (group - slot) + 32)
                    for u in range(GU):
                        unit(n + u, u, lambda j: vh[:, slot, :, u * UNIT + j, :])
                groups(pe, rows, columns)

            def phase_b(half, with_a):
                pe.wait_ge(wo_loaded, 2 * 16)
                pe.wait_ge(conv_out, HALF_UNITS * (half + 1))
                pe.wait_ge(rows_set, 2 + 3 * (half + 1))

                transpose_x(xs_b(half, 0), xn_b[:, 0])

                def body(c, first, last):
                    for r in range(CH):
                        t = CH * c + r
                        m = STEPS * half + t
                        more = not (last and r == CH - 1)
                        transpose_y(half, t, r)
                        if with_a:
                            transpose_x(xs_a(1, t), x_a[:, r % 2])
                        elif more:
                            transpose_x(xs_b(half, t + 1), xn_b[:, (r + 1) % 2])
                        project_u(half, t, xs_b(half, t), 0 if with_a else r)
                        if not first or r > 0:
                            project_out(m - 1, r - 1)
                        if with_a:
                            if more:
                                transpose_x(xs_b(half, t + 1), xn_b[:, (r + 1) % 2])
                            project_v(1, t, xs_a(1, t), 1)
                chunks(pe, body)
                project_out(STEPS * half + STEPS - 1, CH - 1)

            phase_c(0)
            phase_b(0, True)
            phase_c(1)
            phase_b(1, False)


def kernel(**inputs):
    import numpy as _np
    import concourse.bacc as _bacc
    from concourse import mybir as _mybir
    from concourse.bass_utils import run_bass_kernel_spmd as _run

    get = {k.replace("L0_conv_", ""): _np.asarray(a) for k, a in inputs.items()}
    both = lambda name: _np.stack([get["rpe1_" + name], get["rpe2_" + name]])
    x = get["x"].reshape(HALVES, NB, STEPS, 2, WIDTH, E).transpose(0, 2, 3, 4, 1, 5)
    arrays = {
        "x": x.reshape(ALL_STEPS, P, NB * E),
        "u_wT": get["u_w"].T, "u_b": get["u_b"].reshape(1, D),
        "v_wT": get["v_w"].T, "v_b": get["v_b"].reshape(1, D),
        "o_wT": get["o_w"].T, "o_b": get["o_b"].reshape(1, E),
        "pos_w": both("pos_w").reshape(2, RC, P).transpose(2, 0, 1),
        "pos_b": both("pos_b").reshape(2, RC, P).transpose(2, 0, 1),
        "lwT": both("lw").transpose(0, 1, 3, 2), "lb": both("lb").reshape(2, LAYERS, RC, P).transpose(3, 0, 1, 2),
        "out_wT": both("out_w").transpose(0, 2, 1), "out_b": both("out_b"),
    }
    nc = _bacc.Bacc("TRN2", target_bir_lowering=False, num_devices=1)
    ins, args = {}, []
    for name, a in arrays.items():
        a = _np.ascontiguousarray(a)
        ins[f"in_{name}"] = a
        args.append(nc.dram_tensor(f"in_{name}", a.shape, _mybir.dt.from_np(a.dtype), kind="ExternalInput").ap())
    args.append(nc.dram_tensor("out_0", (ALL_STEPS, P, NB * E), _mybir.dt.float32, kind="ExternalOutput").ap())
    tno_kernel(nc, *args)
    r = _run(nc, [ins], core_ids=[0])
    y = _np.asarray(r.results[0]["out_0"]).reshape(HALVES, STEPS, 2, WIDTH, NB, E)
    return _np.ascontiguousarray(y.transpose(0, 4, 1, 2, 3, 5)).reshape(IMAGES, HEIGHT, WIDTH, E)
```

```python
import itertools

import concourse.bass as bass
from concourse import mybir
from contextlib import ExitStack

IMAGES, HEIGHT, WIDTH, E = 8, 64, 64, 96
D = 288
RPE, LAYERS = 256, 3
EPS = 1e-8
P = 128
NB = 4
STEPS = HEIGHT // 2
HALVES = IMAGES // NB
ALL_STEPS = HALVES * STEPS
KE = E + 1
NCH = D // E
GROUP = 32
GROUPS = D // GROUP
UNIT = 8
GU = GROUP // UNIT
UNITS = D // UNIT
HALF_UNITS = 2 * UNITS
TAIL = GU + 2 * GU * (GROUPS - 3)
RC = RPE // P
TOK = NB * P
CH = 4
NORM_STEPS = 2
ROOT_GUESS = 0x1FBD1DF5
EARLY = (GROUPS - 1) * GROUP
LAG_V, LAG_O = 2, 3


def tno_kernel(nc, x, x_eT, u_wT, u_b, v_wT, v_b, o_wT, o_b, pos_w, pos_b, lwT, lb, out_wT, out_b, out):
    f32, f32r, i32 = mybir.dt.float32, mybir.dt.float32r, mybir.dt.int32
    ALU, ACT, AX = mybir.AluOpType, mybir.ActivationFunctionType, mybir.AxisListType

    ctx = ExitStack()
    with ctx:
        base = -(-nc.sbuf_base // 32) * 32

        def place(name, shape, offset, dtype=f32):
            return nc.alloc_sbuf_tensor_at(name, shape, dtype, offset=base + offset)

        V_BYTES = STEPS * D * NB * 4
        v = place("v", [P, STEPS, D, NB], 0)
        w_raw = place("w_raw", [KE, 2, D], 0)
        x_all = place("x_all", [P, STEPS, NB, E], V_BYTES - STEPS * NB * E * 4)
        HB = STEPS * GROUP * NB * 4
        vh = place("vh", [P, 2, STEPS, GROUP, NB], V_BYTES)
        toep = place("toep", [P, GU, UNIT, P], V_BYTES + 2 * HB)
        stage = place("stage", [P, 96 * UNIT], V_BYTES + 2 * HB + 17408)
        region_end = V_BYTES + 2 * HB + 16384 + 4096
        ysum_b = place("ysum_b", [P, D, NB], V_BYTES)
        x_b1 = place("x_b1", [P, NB, E], V_BYTES + 4608)
        x_e = place("x_e", [E, CH, TOK], V_BYTES + 6144)
        ysum = [place("ysum_a", [P, D, NB], V_BYTES + 16384), ysum_b]
        x_b = [place("x_b0", [P, NB, E], V_BYTES + 20992), x_b1]
        xh = place("xh", [KE, 2, TOK], V_BYTES + 23552, f32r)
        xl = place("xl", [KE, 2, TOK], V_BYTES + 27648, f32r)
        g = place("g", [KE, 2, NCH, TOK], V_BYTES + 31744, f32r)
        ut = place("ut", [E, NCH, TOK], V_BYTES + 44032)
        x_a = place("x_a", [P, 2, NB, E], V_BYTES + 50176)
        x_a0 = place("x_a0", [P, CH, NB, E], V_BYTES)
        x_sq = place("x_sq", [P, CH * NB, E], V_BYTES + 31744)
        r_lw = place("r_lw", [P, 2, LAYERS, RC, RPE], V_BYTES + 6144)
        r_ow = place("r_ow", [P, 2, RC, D], V_BYTES + 18432)
        R = V_BYTES + 33280
        r_pos = place("r_pos", [P, P], R + 4608)
        r_ones = place("r_ones", [P, P], R + 5120)
        r_h = place("r_h", [P, 2, RC, P], R + 5632)
        r_sq = place("r_sq", [P, 2, RC, P], R + 7680)
        r_in = place("r_in", [P, 2, RC, P], R + 9728)
        r_diag = place("r_diag", [P, 2, P], R + 11776)
        r_a = place("r_a", [P, 2, D], R + 12800)
        r_ob = place("r_ob", [1, 2, D], R + 15104)
        r_posi = place("r_posi", [P, P], R + 17408, i32)
        r_pw = place("r_pw", [P, 2, 2, RC], R + 17920)
        r_lb = place("r_lb", [P, 2, LAYERS, RC], R + 17952)
        wv = place("wv", [KE, 2, D], region_end, f32r)
        wu = place("wu", [KE, 2, D], region_end + 2304, f32r)
        wo = place("wo", [KE, 2, NCH, E], region_end + 4608, f32r)
        ident = place("ident", [P, P], region_end + 6912)
        rn = place("rn", [P, ALL_STEPS * NB], region_end + 7424)
        x_n = place("x_n", [P, NORM_STEPS * NB, E], region_end + 8448)
        n_tmp = place("n_tmp", [P, 3, CH * NB + 2], region_end + 11520)
        assert base + region_end + 11744 <= nc.sbuf_usable_end
        wo_raw = place("wo_raw", [KE, NCH, E], region_end + 8448)

        ps = ctx.enter_context(nc.psum_tensor("ps", [P, 8, 512], f32))
        V_BANK = [0, 2]
        U_BANK = [0, 1, 2]
        Y_BANK = [4, 5, 3]
        X_BANK, O_BANK = 6, 7

        v_dram = nc.dram_tensor("v_dram", (HALVES, STEPS, P, D * NB), f32, kind="Internal").ap()
        y_dram = nc.dram_tensor("y_dram", (HALVES, STEPS, P, D * NB), f32, kind="Internal").ap()
        a_dram = nc.dram_tensor("a_dram", (2, UNITS, P, UNIT), f32, kind="Internal").ap()

        def by_column(dram, half):
            return dram[half].rearrange("t (q k w) m -> k (t q) w m", q=2, k=2)

        def sem(name):
            return ctx.enter_context(nc.semaphore(name))

        x_all_loaded = sem("x_all_loaded")
        weights_loaded, wo_loaded, wo_split = sem("weights_loaded"), sem("wo_loaded"), sem("wo_split")
        w_split = sem("w_split")
        pos_loaded, rpe_loaded = sem("pos_loaded"), sem("rpe_loaded")
        zeroed, consts_ready, positions = sem("zeroed"), sem("consts_ready"), sem("positions")
        dve_chain, norm_chain = sem("dve_chain"), sem("norm_chain")
        rpe_squared, rpe_summed, rpe_diag = sem("rpe_squared"), sem("rpe_summed"), sem("rpe_diag")
        rpe_spread, rpe_normed, rpe_layer = sem("rpe_spread"), sem("rpe_normed"), sem("rpe_layer")
        a_ready, a_stored = sem("a_ready"), sem("a_stored")
        xn_loaded, squared, norms_summed, norms_ready = (
            sem("xn_loaded"), sem("squared"), sem("norms_summed"), sem("norms_ready"))
        xa_loaded = [sem(f"xa_loaded{k}") for k in range(2)]
        xb_loaded = [sem(f"xb_loaded{k}") for k in range(2)]
        xe_loaded = [sem(f"xe_loaded{k}") for k in range(CH)]
        x_scaled, x_transposed, xh_ready, xl_ready = (
            sem("x_scaled"), sem("x_transposed"), sem("xh_ready"), sem("xl_ready"))
        x_projected = sem("x_projected")
        rows_set = sem("rows_set")
        v_first = sem("v_first")
        v_ready, v_stored = sem("v_ready"), sem("v_stored")
        u_part, u_ready = sem("u_part"), sem("u_ready")
        ysum_loaded = [sem(f"ysum_loaded{k}") for k in range(2)]
        ysum_ready, y_transposed, g_ready = sem("ysum_ready"), sem("y_transposed"), sem("g_ready")
        gh_ready, gl_ready = sem("gh_ready"), sem("gl_ready")
        o_projected, o_ready = sem("o_projected"), sem("o_ready")
        o_stored = [sem(f"o_stored{k}") for k in range(CH)]
        stage_loaded = [sem(f"stage_loaded{k}") for k in range(GU)]
        toep_zeroed, toep_ready = sem("toep_zeroed"), sem("toep_ready")
        vh_loaded = [sem(f"vh_loaded{k}") for k in range(2)]
        conv_done, conv_out = sem("conv_done"), sem("conv_out")
        yh_stored = [sem(f"yh_stored{k}") for k in range(2)]

        def wait(engine, semaphore, count):
            if isinstance(count, int) and count <= 0:
                return
            engine.wait_ge(semaphore, count)

        def xs_a(half, t):
            return t if half == 0 else STEPS + 1 + 2 * t

        def xs_b(half, t):
            return STEPS + 2 * t if half == 0 else 3 * STEPS + t

        def chunks(engine, body, alone=1, after=None, tail=1):
            for c in range(alone):
                body(c, c == 0, False)
            if after:
                after()
            with engine.Fori(alone, STEPS // CH - tail) as c:
                body(c, False, False)
            for c in range(STEPS // CH - tail, STEPS // CH):
                body(c, False, c == STEPS // CH - 1)

        def groups(engine, row_block, column_block):
            row_block(0, 0)
            with engine.Fori(0, (GROUPS - 3) // 2) as i:
                for k in range(2):
                    row_block(2 * i + (k + 1), GU + 2 * GU * (2 * i + k))
                    column_block(2 * i + k, k, 2 * GU + 2 * GU * (2 * i + k))
            row_block(GROUPS - 2, TAIL)
            for k in range(3):
                column_block(GROUPS - 3 + k, k % 2, TAIL + GU * (1 + k))
            row_block(GROUPS - 1, TAIL + 4 * GU)

        block = ctx.enter_context(nc.Block())

        @block.sync
        def _(sp):
            def load_x_all(c):
                wait(sp, x_all_loaded, 16 * c)
                sp.dma_start(x_all[:, CH * c:CH * (c + 1)].rearrange("p s n e -> p s (n e)"),
                             x[CH * c:CH * (c + 1)].rearrange("s p m -> p s m")).then_inc(x_all_loaded, 16)

            load_x_all(0)
            sp.dma_start(r_pw[:, 0], pos_w).then_inc(pos_loaded, 16)
            sp.dma_start(r_pw[:, 1], pos_b).then_inc(pos_loaded, 16)
            sp.dma_start(w_raw[0:E, 0], v_wT).then_inc(weights_loaded, 16)
            sp.dma_start(w_raw[E:KE, 0], v_b).then_inc(weights_loaded, 16)
            sp.dma_start(w_raw[0:E, 1], u_wT).then_inc(weights_loaded, 16)
            sp.dma_start(w_raw[E:KE, 1], u_b).then_inc(weights_loaded, 16)
            load_x_all(1)
            sp.dma_start(r_lb[:], lb).then_inc(rpe_loaded, 16)
            for n in range(2):
                sp.dma_start(r_lw[:, n], lwT[n].rearrange("l (c p) o -> p l c o", p=P)).then_inc(rpe_loaded, 16)
                sp.dma_start(r_ow[:, n], out_wT[n].rearrange("(c p) o -> p c o", p=P)).then_inc(rpe_loaded, 16)
                sp.dma_start(r_ob[0:1, n], out_b[n:n + 1, :]).then_inc(rpe_loaded, 16)
            for c in range(2, STEPS // CH):
                load_x_all(c)
            sp.dma_start(wo_raw[0:E], o_wT.rearrange("(k c) e -> c k e", c=E)).then_inc(wo_loaded, 16)
            sp.dma_start(wo_raw[E:KE, 0], o_b).then_inc(wo_loaded, 16)

            def store_a():
                sp.wait_ge(a_ready, 2)
                for n in range(2):
                    sp.dma_start(a_dram[n].rearrange("u k c -> k u c"),
                                 r_a[:, n].rearrange("p (u c) -> p u c", c=UNIT)).then_inc(a_stored, 16)

            def load_a(t, r):
                sp.dma_start(x_a[:, r % 2].rearrange("p n e -> p (n e)"),
                             x[bass.ds(STEPS + t, 1)].rearrange("s p m -> p (s m)")).then_inc(xa_loaded[r % 2], 16)

            def load_norms(j):
                wait(sp, norms_summed, STEPS // CH + j)
                sp.dma_start(x_n[:].rearrange("p (s n) e -> p s (n e)", n=NB),
                             x[bass.ds(STEPS + NORM_STEPS * j, NORM_STEPS)].rearrange("s p m -> p s m")
                             ).then_inc(xn_loaded, 16)

            def store_v(half, t):
                sp.wait_ge(v_ready, 2 * (STEPS * half + t) + 2)
                sp.dma_start(v_dram[half, bass.ds(t, 1)].rearrange("s p m -> p (s m)"),
                             v[:, bass.ds(t, 1)].rearrange("p s c n -> p (s c n)")).then_inc(v_stored, 16)

            def load_xb(half, t, r):
                sp.dma_start(x_b[r % 2].rearrange("p n e -> p (n e)"),
                             x[bass.ds(STEPS * half + t, 1)].rearrange("s p m -> p (s m)")).then_inc(xb_loaded[r % 2], 16)

            def load_xe(half, t, r):
                sp.dma_start(x_e[:, r], x_eT[bass.ds(STEPS * half + t, 1)].rearrange("s e m -> e (s m)")
                             ).then_inc(xe_loaded[r], 16)

            def load_ysum_part(half, start, end):
                sp.dma_start(ysum[0][:, start:end].rearrange("p c n -> p (c n)"),
                             y_dram[half, 0][:, NB * start:NB * end]).then_inc(ysum_loaded[0], 16)

            def load_ysum(half, t, r):
                sp.dma_start(ysum[r % 2].rearrange("p c n -> p (c n)"),
                             y_dram[half, bass.ds(t, 1)].rearrange("s p m -> p (s m)")).then_inc(ysum_loaded[r % 2], 16)

            def store_out(half, t, r):
                sp.wait_ge(o_ready, STEPS * half + t + 1)
                sp.dma_start(out[bass.ds(STEPS * half + t, 1)].rearrange("s e m -> e (s m)"), x_e[:, r]
                             ).then_inc(o_stored[r], 16)

            def load_toep(half, axis, unit, u, n):
                wait(sp, toep_ready, 4 * (HALF_UNITS * half + n - GU) + 4)
                src = a_dram[axis, bass.ds(unit, 1)].rearrange("u k c -> (u k) c")[0:1]
                runs = bass.AP(src.tensor, src.offset, [[UNIT, 32], [1, 96 * UNIT]])
                sp.dma_start(stage[32 * u:32 * u + 32], runs).then_inc(stage_loaded[u], 16)

            def toeps(half, axis, group, n, units=range(GU)):
                for u in units:
                    load_toep(half, axis, group * GU + u, u, n + u)

            def after_networks():
                store_a()
                sp.wait_ge(a_stored, 32)
                toeps(0, 0, 0, 0)

            def phase_a(c, first, last):
                for r in range(CH):
                    store_v(0, CH * c + r)
            chunks(sp, phase_a, LAYERS + 1, after_networks)
            sp.wait_ge(wo_split, 4)
            load_norms(0)

            def phase_c(half):
                def load_vh(group, slot, k):
                    if not (isinstance(group, int) and group < 2):
                        sp.wait_ge(yh_stored[k], 16 * GROUPS * half + 16 * (group - 1))
                    sp.dma_start(vh[64 * k:64 * k + 64, slot].rearrange("p w c n -> p w (c n)"),
                                 by_column(v_dram, half)[k][:, :, bass.ds(group * (GROUP * NB), GROUP * NB)]
                                 ).then_inc(vh_loaded[slot], 16)

                def store_yh(group, slot, n, k):
                    sp.wait_ge(conv_out, HALF_UNITS * half + n)
                    sp.dma_start(by_column(y_dram, half)[k][:, :, bass.ds(group * (GROUP * NB), GROUP * NB)],
                                 vh[64 * k:64 * k + 64, slot].rearrange("p w c n -> p w (c n)")
                                 ).then_inc(yh_stored[k], 16)

                def turn(group, slot, end, first, second, last=False):
                    early, late = range(GU - 1), range(GU - 1, GU)
                    toeps(half, *first, early)
                    store_yh(group, slot, end, 0)
                    toeps(half, *first, late)
                    store_yh(group, slot, end, 1)
                    if last:
                        early, late = (), range(GU)
                    toeps(half, *second, early)
                    load_vh(group + 2, slot, 0)
                    if last:
                        load_vh(group + 2, slot, 1)
                    toeps(half, *second, late)
                    if not last:
                        load_vh(group + 2, slot, 1)

                def all_stored(count):
                    for k in range(2):
                        sp.wait_ge(yh_stored[k], 16 * (GROUPS * half + count))

                toeps(half, 0, 1, GU)
                sp.wait_ge(v_stored, 16 * STEPS * (half + 1))
                if half:
                    for k in range(CH):
                        sp.wait_ge(o_stored[k], 16 * (STEPS // CH))
                    sp.wait_ge(x_projected, STEPS * 3)
                for k in range(2):
                    load_vh(0, 0, k)
                toeps(half, 1, 0, 2 * GU)
                for k in range(2):
                    load_vh(1, 1, k)
                toeps(half, 0, 2, 3 * GU)

                with sp.Fori(0, (GROUPS - 5) // 2) as i:
                    for k in range(2):
                        n = 3 * GU + 2 * GU * (2 * i + k)
                        turn(2 * i + k, k, n, (1, 2 * i + (k + 1), n + GU), (0, 2 * i + (k + 3), n + 2 * GU))
                turn(GROUPS - 5, 0, TAIL - 2 * GU, (1, GROUPS - 4, TAIL - GU), (0, GROUPS - 2, TAIL))
                turn(GROUPS - 4, 1, TAIL, (1, GROUPS - 3, TAIL + GU), (1, GROUPS - 2, TAIL + 2 * GU))
                turn(GROUPS - 3, 0, TAIL + 2 * GU, (1, GROUPS - 1, TAIL + 3 * GU), (0, GROUPS - 1, TAIL + 4 * GU), True)
                for k in range(2):
                    store_yh(GROUPS - 2, 1, TAIL + 3 * GU, k)
                if half == 0:
                    load_norms(1)
                all_stored(GROUPS - 1)
                load_xb(half, 0, 0)
                load_ysum_part(half, 0, EARLY)
                for k in range(2):
                    store_yh(GROUPS - 1, 0, TAIL + 4 * GU, k)
                if half == 0:
                    sp.wait_ge(toep_ready, 4 * HALF_UNITS)
                    load_a(0, 0)
                    load_a(1, 1)
                all_stored(GROUPS)
                load_ysum_part(half, EARLY, D)

            def phase_b(half, with_a):
                def body(c, first, last):
                    for r in range(CH):
                        t = CH * c + r
                        if not first or r >= 2:
                            sp.wait_ge(x_transposed, xs_b(half, t) - (3 if half == 0 else 1))
                        if not (first and r == 0):
                            load_xb(half, t, r)
                        if not first or r >= 2:
                            sp.wait_ge(y_transposed, NCH * (STEPS * half + t - 1))
                        if not (first and r == 0):
                            load_ysum(half, t, r)
                        if with_a:
                            if not first or r >= 2:
                                sp.wait_ge(x_transposed, xs_a(1, t) - 3)
                                load_a(t, r)
                            if not first or r >= LAG_V:
                                store_v(1, CH * c + (r - LAG_V))
                        if not first:
                            sp.wait_ge(o_stored[r], 16 * (STEPS // CH) * half + 16 * c)
                        if first and r == 1:
                            load_xe(half, 0, 0)
                        if not (first and r == 0):
                            load_xe(half, t, r)
                        if not first or r >= LAG_O:
                            store_out(half, CH * c + (r - LAG_O), (r - LAG_O) % CH)
                        if with_a and r % 2 and not last:
                            load_norms(2 * c + (r // 2 + 2))
                chunks(sp, body)
                if with_a:
                    store_v(1, STEPS - 2)
                    for t in (STEPS - 3, STEPS - 2):
                        store_out(half, t, t % CH)
                    sp.wait_ge(x_transposed, 3 * STEPS)
                    toeps(1, 0, 0, 0)
                    store_v(1, STEPS - 1)
                    store_out(half, STEPS - 1, (STEPS - 1) % CH)
                else:
                    for t in range(STEPS - LAG_O, STEPS):
                        store_out(half, t, t % CH)

            phase_c(0)
            phase_b(0, True)
            phase_c(1)
            phase_b(1, False)
            for r in range(CH):
                sp.wait_ge(o_stored[r], 16 * HALVES * STEPS // CH)

        @block.gpsimd
        def _(pool):
            nc.gpsimd.memset(ident[:], 0.0).then_inc(zeroed, 1)
            nc.gpsimd.memset(r_ones[:], 1.0).then_inc(zeroed, 1)
            pool.wait_ge(zeroed, 2)
            nc.gpsimd.affine_select(out=ident[:], in_=ident[:], compare_op=ALU.not_equal, fill=1.0, base=0,
                                    pattern=[[-1, P]], channel_multiplier=1).then_inc(consts_ready, 1)
            nc.gpsimd.iota(r_posi[:], pattern=[[-1, P]], base=WIDTH - 1, channel_multiplier=0).then_inc(positions, 1)
            pool.wait_ge(positions, 1)
            nc.gpsimd.tensor_copy(r_pos[:], r_posi[:]).then_inc(positions, 1)

            def scale(half, t, source, target):
                factor = rn[:, bass.ds((STEPS * half + t) * NB, NB)].unsqueeze(2).to_broadcast([P, NB, E])
                nc.gpsimd.tensor_tensor(out=target, in0=source, in1=factor, op=ALU.mult).then_inc(x_scaled, 1)

            def scale_a0(t, c, r):
                pool.wait_ge(norms_ready, c + 1)
                wait(pool, x_transposed, t - (CH - 1))
                scale(0, t, x_all[:, bass.ds(t, 1)].rearrange("p s n e -> p (s n) e"), x_a0[:, r])

            def scale_a1(t, c, r):
                pool.wait_ge(norms_ready, STEPS // CH + 2 * c + (r // 2 + 1))
                pool.wait_ge(xa_loaded[r % 2], 32 * c + (16 * (r // 2) + 16))
                scale(1, t, x_a[:, r % 2], x_a[:, r % 2])

            def square(source, target):
                nc.gpsimd.tensor_tensor(out=target, in0=source, in1=source, op=ALU.mult).then_inc(squared, 1)

            def square_a0(c, r):
                if r == 0:
                    pool.wait_ge(x_all_loaded, 16 * (c + 1))
                    wait(pool, norms_summed, c)
                square(x_all[:, bass.ds(CH * c + r, 1)].rearrange("p s n e -> p (s n) e"),
                       x_sq[:, NB * r:NB * (r + 1)])

            def square_a1(j):
                pool.wait_ge(xn_loaded, 16 * (j + 1))
                square(x_n[:], x_n[:])

            def scale_b(half, t, c, r):
                pool.wait_ge(xb_loaded[r % 2], 16 * (STEPS // 2) * half + 32 * c + (16 * (r // 2) + 16))
                scale(half, t, x_b[r % 2][:], x_b[r % 2][:])

            for r in range(2):
                square_a0(0, r)
            for r in range(CH - 2):
                square_a0(1, r)

            def phase_a(c, first, last):
                for r in range(CH):
                    scale_a0(CH * c + r, c, r)
                    if first and r == 0:
                        square_a0(1, CH - 2)
                        square_a0(1, CH - 1)
                    if not (isinstance(c, int) and c >= STEPS // CH - 2):
                        for k in ((), (0,), (1,), (2, 3))[r]:
                            square_a0(c + 2, k)
            chunks(pool, phase_a, tail=2)

            def zero_toep(half):
                for u in range(GU):
                    if half and u == GU - 1:
                        pool.wait_ge(gl_ready, NCH * STEPS)
                    for k in range(2):
                        nc.gpsimd.memset(toep[64 * k:64 * k + 64, u, :, 64 - 64 * k:P - 64 * k], 0.0).then_inc(toep_zeroed, 1)
                        pool.wait_ge(toep_zeroed, 2 * GU * half + 2 * u + k + 1)

            pool.wait_ge(a_stored, 32)
            pool.wait_ge(norms_summed, STEPS // CH)
            pool.wait_ge(x_scaled, STEPS)
            zero_toep(0)
            square_a1(0)
            square_a1(1)

            def phase_b(half, with_a):
                for k in range(2):
                    pool.wait_ge(yh_stored[k], 16 * (GROUPS * half + GROUPS - 1))
                if half == 0:
                    pool.wait_ge(squared, CH * (STEPS // CH) + 2)
                n = 2 + 4 * half
                nc.gpsimd.memset(xh[E:KE].bitcast(f32), 1.0).then_inc(rows_set, 1)
                pool.wait_ge(rows_set, n + 1)
                nc.gpsimd.memset(xl[E:KE].bitcast(f32), 0.0).then_inc(rows_set, 1)
                pool.wait_ge(rows_set, n + 2)
                scale_b(half, 0, 0, 0)
                pool.wait_ge(x_scaled, xs_b(half, 0) + 1)

                def add_first(start, end, part):
                    pool.wait_ge(ysum_loaded[0], (16 * (STEPS // 2) + 16) * half + 16 * part)
                    nc.gpsimd.tensor_tensor(out=ysum[0][:, start:end], in0=ysum[0][:, start:end], in1=v[:, 0, start:end],
                                            op=ALU.add).then_inc(ysum_ready, 1)

                add_first(0, EARLY, 1)
                pool.wait_ge(ysum_ready, (STEPS + 1) * half + 1)
                pool.wait_ge(conv_done, HALF_UNITS * (half + 1))
                for k, value in enumerate((1.0, 0.0)):
                    nc.gpsimd.memset(g[E:KE, k, 0].bitcast(f32), value).then_inc(rows_set, 1)
                    pool.wait_ge(rows_set, n + 3 + k)
                if with_a:
                    scale_a1(0, 0, 0)
                pool.wait_ge(conv_out, HALF_UNITS * (half + 1))
                add_first(EARLY, D, 2)

                def body(c, first, last):
                    for r in range(CH):
                        t = CH * c + r
                        if not (first and r == 0):
                            pool.wait_ge(ysum_loaded[r % 2], (16 * (STEPS // 2) + 16 * (r % 2 == 0)) * half
                                         + 32 * c + (16 * (r // 2) + 16 + 16 * (r % 2 == 0)))
                            nc.gpsimd.tensor_tensor(out=ysum[r % 2].rearrange("p c n -> p (c n)"),
                                                    in0=ysum[r % 2].rearrange("p c n -> p (c n)"),
                                                    in1=v[:, bass.ds(t, 1)].rearrange("p s c n -> p (s c n)"),
                                                    op=ALU.add).then_inc(ysum_ready, 1)
                        if with_a:
                            if not (first and r == 0):
                                scale_a1(t, c, r)
                        if r < CH - 1:
                            scale_b(half, t + 1, c, r + 1)
                        elif not last:
                            scale_b(half, t + 1, c + 1, 0)
                        if with_a and r % 2 and not last:
                            square_a1(2 * c + (r // 2 + 2))
                chunks(pool, body)
            phase_b(0, True)
            pool.wait_ge(o_projected, STEPS)
            pool.wait_ge(x_scaled, 3 * STEPS)
            zero_toep(1)
            phase_b(1, False)

        @block.scalar
        def _(act):
            def high(xs, r):
                act.wait_ge(x_transposed, xs + 1)
                wait(act, x_projected, xs - 1)
                nc.scalar.copy(xh[0:E, r % 2], ps[0:E, X_BANK]).then_inc(xh_ready, 1)

            def silu_v(half, t, xs):
                for q in range(2):
                    if q == 0:
                        act.wait_ge(v_first, STEPS * half + t + 1)
                        if half:
                            act.wait_ge(ysum_ready, t + 2)
                    else:
                        act.wait_ge(x_projected, xs + 1)
                    nc.scalar.activation(
                        v[:, bass.ds(t, 1), :, 2 * q:2 * q + 2].rearrange("p s c n -> p (s c) n"),
                        ps[:, V_BANK[q]:V_BANK[q] + 2, 0:D].rearrange("p n c -> p c n"),
                        ACT.Silu).then_inc(v_ready, 1)

            def silu_u(half, t, xs):
                for k in range(NCH):
                    if k < NCH - 1:
                        act.wait_ge(u_part, (NCH - 1) * (STEPS * half + t) + (k + 1))
                    else:
                        act.wait_ge(x_projected, xs + 1)
                    wait(act, gl_ready, NCH * (STEPS * half + t) - (NCH - 1 - k))
                    nc.scalar.activation(ut[:, k], ps[0:E, U_BANK[k]], ACT.Silu).then_inc(u_ready, 1)

            def high_g(m, which=range(NCH)):
                wait(act, o_projected, m)
                for k in which:
                    act.wait_ge(g_ready, NCH * m + (k + 1))
                    nc.scalar.copy(g[0:E, 0, k], ut[:, k]).then_inc(gh_ready, 1)

            high(xs_a(0, 0), 0)

            def phase_a(c, first, last):
                for r in range(CH):
                    t = CH * c + r
                    if not (last and r == CH - 1):
                        high(xs_a(0, t + 1), r + 1)
                    silu_v(0, t, xs_a(0, t))
            chunks(act, phase_a)

            def phase_c(half):
                act.wait_ge(v_stored, 16 * STEPS * (half + 1))

                def evacuate(n, u, target):
                    act.wait_ge(conv_done, HALF_UNITS * half + n + 1)
                    nc.scalar.copy(target, ps[:, 2 * u:2 * u + 2].rearrange(
                        "p k (c t n) -> p t (k c) n", c=NB, t=STEPS)).then_inc(conv_out, 1)

                def rows(group, n):
                    for u in range(GU):
                        if isinstance(group, int) and group == GROUPS - 1 and u == GU - 2:
                            high(xs_b(half, 0), 0)
                        evacuate(n + u, u, v[:, :, bass.ds(group * GROUP + u * UNIT, UNIT), :])

                def columns(group, slot, n):
                    for u in range(GU):
                        evacuate(n + u, u, vh[:, slot, :, u * UNIT:(u + 1) * UNIT, :])
                groups(act, rows, columns)

            def phase_b(half, with_a):
                def body(c, first, last):
                    for r in range(CH):
                        t = CH * c + r
                        more = not (last and r == CH - 1)
                        if with_a:
                            high(xs_a(1, t), 1)
                            silu_u(half, t, xs_b(half, t))
                            high_g(STEPS * half + t, (0,))
                            if more:
                                high(xs_b(half, t + 1), 0)
                            high_g(STEPS * half + t, (1,) if more else (1, 2))
                            silu_v(1, t, xs_a(1, t))
                            if more:
                                high_g(STEPS * half + t, (2,))
                        else:
                            if more:
                                high(xs_b(half, t + 1), r + 1)
                            silu_u(half, t, xs_b(half, t))
                            high_g(STEPS * half + t)
                chunks(act, body)
            phase_c(0)
            phase_b(0, True)
            phase_c(1)
            phase_b(1, False)

        @block.vector
        def _(dve):
            links = [0]

            def link(instruction):
                links[0] += 1
                instruction.then_inc(dve_chain, 1)
                dve.wait_ge(dve_chain, links[0])

            def inverse(total, root, inv):
                ts, stt = nc.vector.tensor_scalar, nc.vector.scalar_tensor_tensor
                steps = [lambda: ts(root.bitcast(i32), total.bitcast(i32), 1, None, ALU.logical_shift_right),
                         lambda: ts(root.bitcast(i32), root.bitcast(i32), float(ROOT_GUESS), None, ALU.add)]
                for _ in range(3):
                    steps += [lambda: nc.vector.reciprocal(inv, root),
                              lambda: stt(out=inv, in0=inv, scalar=0.5, in1=total, op0=ALU.mult, op1=ALU.mult),
                              lambda: stt(out=root, in0=root, scalar=0.5, in1=inv, op0=ALU.mult, op1=ALU.add)]
                return steps + [lambda: ts(root, root, EPS, None, ALU.add)]

            nc.vector.memset(xh[E:KE].bitcast(f32), 1.0).then_inc(rows_set, 1)
            nc.vector.memset(xl[E:KE].bitcast(f32), 0.0).then_inc(rows_set, 1)

            dve.wait_ge(x_all_loaded, 16)
            for r in (2, 3):
                nc.vector.tensor_tensor(out=x_sq[:, NB * r:NB * (r + 1)], in0=x_all[:, r], in1=x_all[:, r],
                                        op=ALU.mult).then_inc(squared, 1)

            dve.wait_ge(pos_loaded, 2 * 16)
            dve.wait_ge(positions, 2)
            for n in range(2):
                for c in range(RC):
                    last = nc.vector.tensor_scalar(r_h[:, n, c], r_pos[:], r_pw[:, 0, n, c:c + 1],
                                                   r_pw[:, 1, n, c:c + 1], ALU.mult, ALU.add)
            link(last)

            def norms(first_step, steps, batch, layer=None):
                cols = steps * NB
                wide = cols if layer is None else cols + 2
                total, root, inv = (n_tmp[:, k, 0:wide] for k in range(3))
                small = [lambda: nc.vector.tensor_scalar(total[:, 0:cols], total[:, 0:cols], 1.0 / E, None, ALU.mult)]
                small += inverse(total, root, inv)
                small += [lambda: nc.vector.reciprocal(rn[:, bass.ds(first_step * NB, cols)], root[:, 0:cols])]
                links = len(small) - 1

                def piece(k):
                    if k == 0:
                        dve.wait_ge(norms_summed, batch + 1)
                        if layer is not None:
                            dve.wait_ge(rpe_summed, layer + 1)
                            nc.vector.tensor_scalar(total[:, cols:wide], ps[:, 7, 0:2 * P:P], 1.0 / RPE, None, ALU.mult)
                    else:
                        dve.wait_ge(norm_chain, links * batch + k)
                    small[k]().then_inc(norm_chain if k < links else norms_ready, 1)
                    if k == links and layer is not None:
                        link(nc.vector.reciprocal(inv[:, cols:wide], root[:, cols:wide]))
                        for n in range(2):
                            nc.vector.tensor_scalar(r_diag[:, n], ident[:], inv[:, cols + n:cols + n + 1], None,
                                                    ALU.mult).then_inc(rpe_diag, 1)
                return [lambda k=k: piece(k) for k in range(len(small))]

            def sum_squares(steps, x2, batch, squares):
                dve.wait_ge(squared, squares)
                nc.vector.reduce_sum(n_tmp[:, 0, 0:steps * NB], x2, axis=AX.X).then_inc(norms_summed, 1)

            def sum_a0(c):
                sum_squares(CH, x_sq[:], c, CH * (c + 1))

            def sum_a1(j):
                sum_squares(NORM_STEPS, x_n[:], STEPS // CH + j, CH * (STEPS // CH) + j + 1)

            def norms_a0(c, layer=None):
                return norms(CH * c, CH, c, layer)

            def norms_a1(j):
                return norms(STEPS + NORM_STEPS * j, NORM_STEPS, STEPS // CH + j)

            def run(pieces):
                for piece in pieces:
                    piece()

            def rpe_square():
                nc.vector.tensor_tensor(out=r_sq[:], in0=r_h[:], in1=r_h[:], op=ALU.mult).then_inc(rpe_squared, 1)

            def rpe_norm(layer):
                dve.wait_ge(rpe_spread, layer + 1)
                for c in range(RC):
                    nc.vector.scalar_tensor_tensor(out=r_in[:, :, c], in0=r_h[:, :, c], scalar=0.0,
                                                   in1=ps[:, 4, 0:2 * P].rearrange("p (n k) -> p n k", n=2),
                                                   op0=ALU.max, op1=ALU.mult).then_inc(rpe_normed, 1)

            def rpe_finish(layer):
                if layer == 0:
                    dve.wait_ge(rpe_loaded, 7 * 16)
                dve.wait_ge(rpe_layer, layer + 1)
                for n in range(2):
                    if layer == LAYERS:
                        nc.vector.tensor_copy(r_a[:, n], ps[:, 4 + n, 0:D]).then_inc(a_ready, 1)
                    else:
                        for c in range(RC):
                            last = nc.vector.tensor_scalar(
                                r_h[:, n, c], ps[:, 5, (RC * n + c) * P:(RC * n + c + 1) * P],
                                r_lb[:, n, layer, c:c + 1], None, ALU.add)
                if layer < LAYERS:
                    link(last)
                    rpe_square()

            def low(xs, r):
                dve.wait_ge(xh_ready, xs + 1)
                nc.vector.tensor_tensor(out=xl[0:E, r % 2], in0=ps[0:E, X_BANK], in1=xh[0:E, r % 2].bitcast(f32),
                                        op=ALU.subtract).then_inc(xl_ready, 1)

            sum_a0(0)
            run(norms_a0(0))
            rpe_square()

            dve.wait_ge(weights_loaded, 4 * 16)
            for n, w in enumerate((wv, wu)):
                nc.vector.tensor_copy(w[:, 0], w_raw[:, n]).then_inc(w_split, 1)
                dve.wait_ge(w_split, 2 * n + 1)
                nc.vector.tensor_tensor(out=w[:, 1], in0=w_raw[:, n], in1=w[:, 0].bitcast(f32), op=ALU.subtract
                                        ).then_inc(w_split, 1)
            low(xs_a(0, 0), 0)

            def phase_a(c, first, last):
                networks = isinstance(c, int) and c <= LAYERS
                for r in range(CH):
                    if not (last and r == CH - 1):
                        low(xs_a(0, CH * c + (r + 1)), r + 1)
                    if r == 0 and not last:
                        pieces = norms_a0(c + 1, c if networks else None)
                    if r < 2 and not last:
                        half_way = len(pieces) // 2
                        run(pieces[half_way * r:half_way * (r + 1)])
                    if networks and r == 2:
                        rpe_norm(c)
                    if networks and r == 3:
                        rpe_finish(c)
                    if r == 3 and not (isinstance(c, int) and c >= STEPS // CH - 2):
                        sum_a0(c + 2)
            sum_a0(1)
            chunks(dve, phase_a, LAYERS + 1, tail=2)

            dve.wait_ge(wo_loaded, 2 * 16)
            for n, (w, raw) in enumerate(((wo[0:E], wo_raw[0:E]), (wo[E:KE, :, 0:1], wo_raw[E:KE, 0:1]))):
                nc.vector.tensor_copy(w[:, 0], raw).then_inc(wo_split, 1)
                dve.wait_ge(wo_split, 2 * n + 1)
                nc.vector.tensor_tensor(out=w[:, 1], in0=raw, in1=w[:, 0].bitcast(f32), op=ALU.subtract).then_inc(wo_split, 1)

            def phase_c(half):
                def pair(u, n, count):
                    dve.wait_ge(stage_loaded[u], count)
                    wait(dve, conv_done, HALF_UNITS * half + n - GU + 1)
                    for k in range(2):
                        for q in range(2):
                            rows = 64 * k + 32 * q
                            nc.vector.tensor_copy(
                                toep[rows:rows + 32, u, :, 64 * k:64 * k + 64],
                                stage[32 * u:32 * u + 32, 32 * q * UNIT:(32 * q + 64) * UNIT].rearrange(
                                    "p (i c) -> p c i", c=UNIT)[:, :, ::-1]).then_inc(toep_ready, 1)

                def loads(n):
                    return 16 * (2 * GROUPS * half) + (16 // GU) * n + 16

                def rows(group, n):
                    for u in range(GU):
                        pair(u, n + u, loads(n))
                    if half == 0 and isinstance(group, int) and group == GROUPS - 2:
                        sum_a1(0)
                        run(norms_a1(0))

                def columns(group, slot, n):
                    for u in range(GU):
                        pair(u, n + u, loads(n))
                groups(dve, rows, columns)

            def phase_b(half, with_a):
                def body(c, first, last):
                    for r in range(CH):
                        t = CH * c + r
                        m = STEPS * half + t
                        more = not (last and r == CH - 1)
                        if with_a:
                            low(xs_a(1, t), 1)
                        elif more:
                            low(xs_b(half, t + 1), r + 1)
                        if r % 2 == 0:
                            between = iter(())
                            if with_a and not (last and r == CH - 2):
                                j = 2 * c + (r // 2 + 1)
                                sum_a1(j)
                                between = iter(norms_a1(j))
                        run(itertools.islice(between, 1))
                        for k in range(NCH):
                            dve.wait_ge(u_ready, NCH * m + (k + 1))
                            dve.wait_ge(y_transposed, NCH * m + (k + 1))
                            nc.vector.tensor_tensor(out=ut[:, k], in0=ps[0:E, Y_BANK[k]], in1=ut[:, k],
                                                    op=ALU.mult).then_inc(g_ready, 1)
                            run(itertools.islice(between, 1 + k // 2))
                        if not first or r > 0:
                            add_x(half, c - (r == 0), (r - 1) % CH)
                        run(itertools.islice(between, 2))
                        for k in range(NCH):
                            dve.wait_ge(gh_ready, NCH * m + (k + 1))
                            nc.vector.tensor_tensor(out=g[0:E, 1, k], in0=ut[:, k], in1=g[0:E, 0, k].bitcast(f32),
                                                    op=ALU.subtract).then_inc(gl_ready, 1)
                            if with_a and more and k == 0:
                                low(xs_b(half, t + 1), 0)
                            run(itertools.islice(between, 1))
                chunks(dve, body)
                add_x(half, STEPS // CH - 1, CH - 1)

            def add_x(half, c, r):
                dve.wait_ge(xe_loaded[r], 16 * (STEPS // CH) * half + 16 * c + 16)
                dve.wait_ge(o_projected, STEPS * half + CH * c + r + 1)
                nc.vector.tensor_tensor(out=x_e[:, r], in0=ps[0:E, O_BANK], in1=x_e[:, r], op=ALU.add).then_inc(o_ready, 1)

            phase_c(0)
            low(xs_b(0, 0), 0)
            phase_b(0, True)
            phase_c(1)
            low(xs_b(1, 0), 0)
            phase_b(1, False)

        @block.tensor
        def _(pe):
            def rpe_part(layer, r):
                if r == 0:
                    if layer == 0:
                        pe.wait_ge(rpe_loaded, 7 * 16)
                        pe.wait_ge(zeroed, 2)
                    pe.wait_ge(rpe_squared, layer + 1)
                    for n in range(2):
                        for c in range(RC):
                            last = nc.tensor.matmul(ps[:, 7, n * P:(n + 1) * P], r_sq[:, n, c], r_ones[:],
                                                    start=(c == 0), stop=(c == RC - 1))
                    last.then_inc(rpe_summed, 1)
                elif r == 2:
                    pe.wait_ge(rpe_diag, 2 * (layer + 1))
                    for n in range(2):
                        last = nc.tensor.matmul(ps[:, 4, n * P:(n + 1) * P], r_ones[:], r_diag[:, n],
                                                start=True, stop=True)
                    last.then_inc(rpe_spread, 1)
                elif r == 3:
                    pe.wait_ge(rpe_normed, RC * (layer + 1))
                    for n in range(2):
                        if layer < LAYERS:
                            for o in range(RC):
                                for c in range(RC):
                                    last = nc.tensor.matmul(ps[:, 5, (RC * n + o) * P:(RC * n + o + 1) * P],
                                                            r_lw[:, n, layer, c, o * P:(o + 1) * P], r_in[:, n, c],
                                                            start=(c == 0), stop=(c == RC - 1))
                        else:
                            for c in range(RC):
                                nc.tensor.matmul(ps[:, 4 + n, 0:D], r_in[:, n, c], r_ow[:, n, c],
                                                 start=(c == 0), stop=False)
                            last = nc.tensor.matmul(ps[:, 4 + n, 0:D], r_ones[0:1], r_ob[0:1, n], start=False, stop=True)
                    last.then_inc(rpe_layer, 1)

            def transpose_x(xs, tile):
                pe.wait_ge(x_scaled, xs + 1)
                wait(pe, xl_ready, xs)
                for n in range(NB):
                    last = nc.tensor.transpose(ps[0:E, X_BANK, n * P:(n + 1) * P], tile[:, n], ident[:])
                last.then_inc(x_transposed, 1)

            SPLIT = ((0, 0), (1, 0), (0, 1))

            def project_v(half, t, xs, r):
                pe.wait_ge(xl_ready, xs + 1)
                if half:
                    m = t + 1
                    pe.wait_ge(u_ready, NCH * m)
                    pe.wait_ge(g_ready, NCH * m)
                for n in range(NB):
                    if n % 2 == 0:
                        wait(pe, v_ready, 2 * (STEPS * half + t) - 1 + n // 2)
                    for k, (xp, wp) in enumerate(SPLIT):
                        last = nc.tensor.matmul(ps[:, V_BANK[n // 2] + n % 2, 0:D], (xh, xl)[xp][:, r % 2, n * P:(n + 1) * P],
                                                wv[:, wp], start=(k == 0), stop=(k == len(SPLIT) - 1))
                    if n % 2:
                        last.then_inc(v_first if n == 1 else x_projected, 1)

            def project_u(half, t, xs, r):
                pe.wait_ge(xl_ready, xs + 1)
                wait(pe, u_ready, NCH * (STEPS * half + t))
                if half == 0:
                    pe.wait_ge(v_ready, 2 * STEPS + 2 * t)
                for k in range(NCH):
                    for s, (xp, wp) in enumerate(SPLIT):
                        last = nc.tensor.matmul(ps[0:E, U_BANK[k]], wu[:, wp, k * E:(k + 1) * E], (xh, xl)[xp][:, r % 2],
                                                start=(s == 0), stop=(s == len(SPLIT) - 1))
                    last.then_inc(u_part if k < NCH - 1 else x_projected, 1)

            def transpose_y(half, t, r, start, which):
                m = STEPS * half + t
                wait(pe, g_ready, NCH * m)
                for k in which:
                    if k == 0 or start and k == NCH - 1:
                        pe.wait_ge(ysum_ready, (STEPS + 1) * half + t + (1 if start and k == 0 else 2))
                    if half == 0 and k == NCH - 1:
                        pe.wait_ge(v_ready, 2 * STEPS + 2 * t)
                    for n in range(NB):
                        last = nc.tensor.transpose(ps[0:E, Y_BANK[k], n * P:(n + 1) * P],
                                                   ysum[r % 2][:, k * E:(k + 1) * E, n], ident[:])
                    last.then_inc(y_transposed, 1)

            def project_out(m):
                wait(pe, o_ready, m)
                for k in range(NCH):
                    pe.wait_ge(gl_ready, NCH * m + (k + 1))
                    rows = KE if k == 0 else E
                    for s, (gp, wp) in enumerate(SPLIT):
                        last = nc.tensor.matmul(ps[0:E, O_BANK], wo[0:rows, wp, k], g[0:rows, gp, k],
                                                start=(k + s == 0), stop=(k == NCH - 1 and s == len(SPLIT) - 1))
                last.then_inc(o_projected, 1)

            pe.wait_ge(consts_ready, 1)

            transpose_x(xs_a(0, 0), x_a0[:, 0])
            pe.wait_ge(rows_set, 2)
            pe.wait_ge(w_split, 4)

            def phase_a(c, first, last):
                for r in range(CH):
                    t = CH * c + r
                    if not (last and r == CH - 1):
                        transpose_x(xs_a(0, t + 1), x_a0[:, (r + 1) % CH])
                    if isinstance(c, int) and c <= LAYERS:
                        rpe_part(c, r)
                    project_v(0, t, xs_a(0, t), r)
            chunks(pe, phase_a, LAYERS + 1)

            def phase_c(half):
                pe.wait_ge(v_ready, 2 * STEPS * (half + 1))

                def unit(n, u, operand):
                    pe.wait_ge(toep_ready, 4 * (HALF_UNITS * half) + 4 * n + 4)
                    wait(pe, conv_out, HALF_UNITS * half + n - GU + 1)
                    for j in range(UNIT):
                        last = nc.tensor.matmul(ps[:, 2 * u + j // NB, (j % NB) * P:(j % NB + 1) * P],
                                                toep[:, u, j], operand(j), start=True, stop=True)
                    last.then_inc(conv_done, 1)

                def rows(group, n):
                    for u in range(GU):
                        if isinstance(group, int) and group == 0:
                            pe.wait_ge(toep_zeroed, 2 * GU * half + 2 * u + 2)
                            if half and u == GU - 1:
                                pe.wait_ge(o_ready, STEPS)
                        if isinstance(group, int) and group == GROUPS - 1:
                            if u == GU - 2:
                                pe.wait_ge(conv_out, HALF_UNITS * half + n)
                                transpose_x(xs_b(half, 0), x_b[0])
                            elif u == GU - 1:
                                pe.wait_ge(xl_ready, xs_b(half, 0) + 1)
                        unit(n + u, u, lambda j: v[:, :, bass.ds(group * GROUP + (u * UNIT + j), 1), :])

                def columns(group, slot, n):
                    loads = -(-GROUPS // 2) if slot == 0 else GROUPS // 2
                    pe.wait_ge(vh_loaded[slot], 32 * loads * half + 16 * (group - slot) + 32)
                    for u in range(GU):
                        unit(n + u, u, lambda j: vh[:, slot, :, u * UNIT + j, :])
                groups(pe, rows, columns)

            def phase_b(half, with_a):
                pe.wait_ge(wo_split, 4)
                pe.wait_ge(conv_out, HALF_UNITS * (half + 1) - 2)
                pe.wait_ge(rows_set, 4 * half + 4)
                project_u(half, 0, xs_b(half, 0), 0)
                pe.wait_ge(conv_out, HALF_UNITS * (half + 1))
                pe.wait_ge(rows_set, 4 * half + 6)

                def body(c, first, last):
                    for r in range(CH):
                        t = CH * c + r
                        m = STEPS * half + t
                        more = not (last and r == CH - 1)
                        transpose_y(half, t, r, first and r == 0, (0, 1))
                        if with_a:
                            transpose_x(xs_a(1, t), x_a[:, r % 2])
                        elif more:
                            transpose_x(xs_b(half, t + 1), x_b[(r + 1) % 2])
                        transpose_y(half, t, r, first and r == 0, (2,))
                        if not (first and r == 0):
                            project_u(half, t, xs_b(half, t), 0 if with_a else r)
                        if not first or r > 0:
                            project_out(m - 1)
                        if with_a:
                            if more:
                                transpose_x(xs_b(half, t + 1), x_b[(r + 1) % 2])
                            project_v(1, t, xs_a(1, t), 1)
                chunks(pe, body)
                project_out(STEPS * half + STEPS - 1)

            phase_c(0)
            phase_b(0, True)
            phase_c(1)
            phase_b(1, False)


def kernel(**inputs):
    import numpy as _np
    import concourse.bacc as _bacc
    from concourse import mybir as _mybir
    from concourse.bass_utils import run_bass_kernel_spmd as _run

    get = {k.replace("L0_conv_", ""): _np.asarray(a) for k, a in inputs.items()}
    both = lambda name: _np.stack([get["rpe1_" + name], get["rpe2_" + name]])
    x = get["x"].reshape(HALVES, NB, STEPS, 2, WIDTH, E).transpose(0, 2, 3, 4, 1, 5)
    arrays = {
        "x": x.reshape(ALL_STEPS, P, NB * E),
        "x_eT": x.transpose(0, 1, 5, 4, 2, 3).reshape(ALL_STEPS, E, TOK),
        "u_wT": get["u_w"].T, "u_b": get["u_b"].reshape(1, D),
        "v_wT": get["v_w"].T, "v_b": get["v_b"].reshape(1, D),
        "o_wT": get["o_w"].T, "o_b": get["o_b"].reshape(1, E),
        "pos_w": both("pos_w").reshape(2, RC, P).transpose(2, 0, 1),
        "pos_b": both("pos_b").reshape(2, RC, P).transpose(2, 0, 1),
        "lwT": both("lw").transpose(0, 1, 3, 2), "lb": both("lb").reshape(2, LAYERS, RC, P).transpose(3, 0, 1, 2),
        "out_wT": both("out_w").transpose(0, 2, 1), "out_b": both("out_b"),
    }
    nc = _bacc.Bacc("TRN2", target_bir_lowering=False, num_devices=1)
    ins, args = {}, []
    for name, a in arrays.items():
        a = _np.ascontiguousarray(a)
        ins[f"in_{name}"] = a
        args.append(nc.dram_tensor(f"in_{name}", a.shape, _mybir.dt.from_np(a.dtype), kind="ExternalInput").ap())
    args.append(nc.dram_tensor("out_0", (ALL_STEPS, E, TOK), _mybir.dt.float32, kind="ExternalOutput").ap())
    tno_kernel(nc, *args)
    r = _run(nc, [ins], core_ids=[0])
    y = _np.asarray(r.results[0]["out_0"]).reshape(HALVES, STEPS, E, NB, 2, WIDTH)
    return _np.ascontiguousarray(y.transpose(0, 3, 1, 4, 5, 2)).reshape(IMAGES, HEIGHT, WIDTH, E)
```
